# Optimizing a Trainium2 kernel written in Bass

```python
import numpy as np
import jax
import jax.numpy as jnp

def _softmax(x, axis=-1):
    return jax.nn.softmax(x, axis=axis)

def _gelu(x):
    return jax.nn.gelu(x, approximate=True)

def _silu(x):
    return jax.nn.silu(x)

def _sigmoid(x):
    return jax.nn.sigmoid(x)

def _layernorm(x, axis=-1, eps=1e-05):
    m = jnp.mean(x, axis=axis, keepdims=True)
    v = jnp.var(x, axis=axis, keepdims=True)
    return (x - m) / jnp.sqrt(v + eps)

def _scatter_add(tgt, idx, src, axis=0):
    return tgt.at[idx].add(src)

def _segment_sum(src, seg, n):
    return jax.ops.segment_sum(src, seg, n)
kernel_name = 'mk_hybrid_d1_jaxref_r8_f8b460'

def setup_inputs(seed: int=0):
    np.random.seed(seed)
    _w = jnp.asarray

    def _L0_attn_a_setup():
        import jax, jax.numpy as jnp
        import numpy as np
        B, S, E, H = (4, 256, 128, 16)
        HD = E // H
        key = jax.random.key(seed)
        ks = jax.random.split(key, 5)
        scale = 1.0 / np.sqrt(E)
        x = jax.random.normal(ks[0], (B, S, E), dtype=jnp.float32)
        Wqkv = jax.random.uniform(ks[1], (E, 3 * E), dtype=jnp.float32, minval=-scale, maxval=scale)
        bqkv = jax.random.uniform(ks[2], (3 * E,), dtype=jnp.float32, minval=-scale, maxval=scale)
        Wout = jax.random.uniform(ks[3], (E, E), dtype=jnp.float32, minval=-scale, maxval=scale)
        bout = jax.random.uniform(ks[4], (E,), dtype=jnp.float32, minval=-scale, maxval=scale)
        return {'x': x, 'Wqkv': Wqkv, 'bqkv': bqkv, 'Wout': Wout, 'bout': bout}
    _L0_attn_a_in = _L0_attn_a_setup()

    def _L0_attn_b_setup():
        import jax, jax.numpy as jnp
        import numpy as np
        B, S, D, H = (2, 256, 128, 16)
        HD = D // H
        key = jax.random.key(seed)
        k1, k2, k3, k4, k5 = jax.random.split(key, 5)
        scale = 1.0 / np.sqrt(D)
        return {'x': jax.random.normal(k1, (B, S, D), dtype=jnp.float32), 'W_qkv': jax.random.normal(k2, (D, 3 * D), dtype=jnp.float32) * scale, 'b_qkv': jax.random.normal(k3, (3 * D,), dtype=jnp.float32) * 0.01, 'W_out': jax.random.normal(k4, (D, D), dtype=jnp.float32) * scale, 'b_out': jax.random.normal(k5, (D,), dtype=jnp.float32) * 0.01}
    _L0_attn_b_in = _L0_attn_b_setup()

    def _L0_ffn_setup():
        import jax, jax.numpy as jnp
        import numpy as np
        DIM = 128
        HIDDEN = 384
        SCALE = 1.0 / 127.0

        def _dequant(w_int, dtype):
            return w_int.astype(dtype) * jnp.asarray(SCALE, dtype)
        key = jax.random.key(seed)
        k_x, k_g, k_u, k_d = jax.random.split(key, 4)
        x = jax.random.normal(k_x, (4, 256, DIM), dtype=jnp.float32)
        w_gate = jax.random.randint(k_g, (HIDDEN, DIM), -127, 128, dtype=jnp.int32)
        w_up = jax.random.randint(k_u, (HIDDEN, DIM), -127, 128, dtype=jnp.int32)
        w_down = jax.random.randint(k_d, (DIM, HIDDEN), -127, 128, dtype=jnp.int32)
        return {'x': x, 'w_gate': w_gate, 'w_up': w_up, 'w_down': w_down}
    _L0_ffn_in = _L0_ffn_setup()
    _d = {'L0_attn_a_x': _L0_attn_a_in['x'], 'L0_attn_a_Wqkv': _L0_attn_a_in['Wqkv'], 'L0_attn_a_bqkv': _L0_attn_a_in['bqkv'], 'L0_attn_a_Wout': _L0_attn_a_in['Wout'], 'L0_attn_a_bout': _L0_attn_a_in['bout'], 'L0_attn_b_W_qkv': _L0_attn_b_in['W_qkv'], 'L0_attn_b_b_qkv': _L0_attn_b_in['b_qkv'], 'L0_attn_b_W_out': _L0_attn_b_in['W_out'], 'L0_attn_b_b_out': _L0_attn_b_in['b_out'], 'L0_ffn_w_gate': _L0_ffn_in['w_gate'], 'L0_ffn_w_up': _L0_ffn_in['w_up'], 'L0_ffn_w_down': _L0_ffn_in['w_down']}
    _x0 = _d['L0_attn_a_x']
    _d['L0_attn_a_x'] = jax.random.normal(jax.random.fold_in(jax.random.key(seed), 1), (4, 1024, 128), dtype=_x0.dtype)
    del _x0
    return _d

def reference(L0_attn_a_x, L0_attn_a_Wqkv, L0_attn_a_bqkv, L0_attn_a_Wout, L0_attn_a_bout, L0_attn_b_W_qkv, L0_attn_b_b_qkv, L0_attn_b_W_out, L0_attn_b_b_out, L0_ffn_w_gate, L0_ffn_w_up, L0_ffn_w_down):

    def _L0_attn_a_ref(x, Wqkv, bqkv, Wout, bout):
        import jax, jax.numpy as jnp
        import numpy as np
        B, S, E, H = (4, 256, 128, 16)
        HD = E // H
        b, s, e = x.shape
        qkv = x @ Wqkv + bqkv
        qkv = qkv.reshape(b, s, H, 3 * HD)
        q, k, v = (qkv[..., :HD], qkv[..., HD:2 * HD], qkv[..., 2 * HD:])
        scores = jnp.einsum('bqhd,bkhd->bhqk', q, k) / jnp.sqrt(jnp.float32(HD))
        attn = jax.nn.softmax(scores, axis=-1)
        out = jnp.einsum('bhqk,bkhd->bqhd', attn, v).reshape(b, s, e)
        return out @ Wout + bout

    def _L0_attn_b_ref(x, W_qkv, b_qkv, W_out, b_out):
        import jax, jax.numpy as jnp
        import numpy as np
        B, S, D, H = (2, 256, 128, 16)
        HD = D // H
        b, s, d = x.shape
        h, hd = (H, HD)
        qkv = (x @ W_qkv + b_qkv).reshape(b, s, h, 3 * hd)
        q = qkv[..., :hd]
        k = qkv[..., hd:2 * hd]
        v = qkv[..., 2 * hd:]
        logits = jnp.einsum('bshd,bkhd->bhsk', q, k) / np.sqrt(hd)
        q_pos = jnp.arange(s)[:, None]
        k_pos = jnp.arange(s)[None, :]
        mask = k_pos > q_pos
        logits = jnp.where(mask[None, None, :, :], -jnp.inf, logits)
        attn = jax.nn.softmax(logits, axis=-1)
        out = jnp.einsum('bhsk,bkhd->bshd', attn, v).reshape(b, s, d)
        return out @ W_out + b_out

    def _L0_ffn_ref(x, w_gate, w_up, w_down):
        import jax, jax.numpy as jnp
        import numpy as np
        DIM = 128
        HIDDEN = 384
        SCALE = 1.0 / 127.0

        def _dequant(w_int, dtype):
            return w_int.astype(dtype) * jnp.asarray(SCALE, dtype)
        wg = _dequant(w_gate, x.dtype)
        wu = _dequant(w_up, x.dtype)
        wd = _dequant(w_down, x.dtype)
        gate = jnp.einsum('bsd,hd->bsh', x, wg)
        up = jnp.einsum('bsd,hd->bsh', x, wu)
        h = jax.nn.silu(gate) * up
        return jnp.einsum('bsh,dh->bsd', h, wd)
    x = L0_attn_a_x
    x = x + _L0_attn_a_ref(_layernorm(x, axis=-1), L0_attn_a_Wqkv, L0_attn_a_bqkv, L0_attn_a_Wout, L0_attn_a_bout)
    x = x + _L0_ffn_ref(_layernorm(x, axis=-1), L0_ffn_w_gate, L0_ffn_w_up, L0_ffn_w_down)
    x = x + _L0_attn_b_ref(_layernorm(x, axis=-1), L0_attn_b_W_qkv, L0_attn_b_b_qkv, L0_attn_b_W_out, L0_attn_b_b_out)
    x = x + _L0_ffn_ref(_layernorm(x, axis=-1), L0_ffn_w_gate, L0_ffn_w_up, L0_ffn_w_down)
    return x

_drawn_inputs = setup_inputs


def setup_inputs(seed=0):
    import zlib

    import numpy as np

    out = dict(_drawn_inputs(seed))
    spreads = {}
    factors = {'L0_attn_b_W_qkv': 8.0,
     'L0_attn_b_b_qkv': 26.108,
     'L0_attn_b_W_out': 8.0,
     'L0_attn_b_b_out': 64.0}
    for name, (base, spread) in spreads.items():
        noise = np.random.default_rng([zlib.crc32(name.encode()), seed]).standard_normal(out[name].shape)
        drawn = base * np.exp(spread * noise) if base else spread * noise
        out[name] = jnp.asarray(drawn.astype(out[name].dtype))
    for name, factor in factors.items():
        out[name] = (out[name] * factor).astype(out[name].dtype)
    return out
```

```python
from contextlib import ExitStack

import concourse.bass as bass
from concourse import mybir
from concourse.alu_op_type import AluOpType as ALU

ACT = mybir.ActivationFunctionType
F32 = mybir.dt.float32
BF16 = mybir.dt.bfloat16
I32 = mybir.dt.int32
AX_X = mybir.AxisListType.X

P = 128
B, S, E, H = 4, 1024, 128, 16
HD = E // H
HIDDEN = 384
FB = HIDDEN // P
EPS = 1e-5
DEQUANT = 1.0 / 127.0
SCORE_SCALE = float(HD) ** -0.5
MASKED = -1.0e30
LOWEST = -3.0e38

TILES = B * S // P
CHUNK = 512
TPC = CHUNK // P
CHUNKS = B * S // CHUNK
KB = S // P
HG = 4
GROUPS = H // HG
WINDOWS = B * GROUPS
PARTS = 3
PD = PARTS * HD
TERMS = PARTS * PD
SHIFT_ROW = 96
SHIFT_PARTS = 2
VH = HD + 1
VW = KB * HG * VH
VPAD = 32 - VH
BUFS = 3
RING = 3
PROBS = 6
SEM_DMA = 16


class Plan:

    def __init__(self, causal, turn, cut_half1, delay):
        self.causal = causal
        self.turn = turn
        self.steps = []
        for f in range(2):
            for j in range(KB):
                c0 = max(0, j * P - f * CHUNK) if causal else 0
                if c0 < CHUNK:
                    self.steps.append((f, j, c0))
        self.n = len(self.steps)
        self.half_start = [0, sum(1 for s in self.steps if s[0] == 0)]
        self.half_end = [self.half_start[1] - 1, self.n - 1]
        halves = []
        for f in range(2):
            units = []
            for qb in range(TPC):
                for c in range(HG):
                    width = (TPC * f + qb + 1) * P if causal else S
                    for kh in range(2):
                        w = min(width - kh * CHUNK, CHUNK)
                        if w > 0:
                            diagonal = causal and kh * CHUNK + w == width
                            units.append(("max", f, c, qb, kh, w, diagonal))
            halves.append(units)
        stream = halves[0] + halves[1]
        at = len(halves[0]) + delay
        stream = stream[:at] + [("shift", 0)] + stream[at:]
        cut = at + 1 + cut_half1
        self.before = [(0, x) for x in stream[:cut]]
        rest = [(0, x) for x in stream[cut:]]
        nxt = [(1, x) for x in stream[:cut]]
        if rest:
            nxt = nxt[:delay] + [(0, ("shift", 1))] + nxt[delay:]
            self.turn_jobs = rest + nxt
        else:
            self.before.append((0, ("shift", 1)))
            self.turn_jobs = nxt + [(1, ("shift", 1))]
        self.turn_steps = [(0, s) for s in range(turn, self.n)] + [(1, s) for s in range(turn)]
        self.turn_plan = self.place(self.turn_jobs, self.turn_steps)
        self.last_plan = [[[x for x in slot if x[0] == 0] for slot in step] for step in self.turn_plan[:self.n - turn]]
        self.last_jobs = [x for step in self.last_plan for slot in step for x in slot]
        self.jobs_before = len(self.before)
        self.jobs_turn = len(self.turn_jobs) + 2
        self.jobs_all = self.jobs_before + (WINDOWS - 1) * self.jobs_turn + len(self.last_jobs) + 1
        self.units = 2 * self.n

    def place(self, jobs, steps):
        cost = [j[5] if j[0] == "max" else P for _, j in jobs]
        slots = [CHUNK - self.steps[s][2] for _, s in steps for _ in range(4)]
        total_c, total_s = max(sum(cost), 1), sum(slots)
        plan, k, done_c, done_s = [], 0, 0, 0
        for i, w in enumerate(slots):
            done_s += w
            slot = []
            while k < len(jobs) and (done_c + cost[k] / 2) * total_s <= done_s * total_c:
                slot.append(jobs[k])
                done_c += cost[k]
                k += 1
            if i == len(slots) - 1:
                slot += jobs[k:]
            plan.append(slot)
        plan = [plan[4 * i: 4 * i + 4] for i in range(len(steps))]
        for i, (dw, s) in enumerate(steps):
            if s == self.half_end[0] + self.turn and dw == 0:
                plan[i][3].append((0, ("norm", 0)))
            if dw == 1 and s == self.turn - 1:
                plan[i][3].append((0, ("norm", 1)))
        return plan


PLANS = [Plan(causal=False, turn=3, cut_half1=16, delay=3), Plan(causal=True, turn=2, cut_half1=99, delay=3)]


def transformer_pair_kernel(nc, x_in, wqkv_a, bqkv_a, wout_a, bout_a, wqkv_b, bqkv_b, wout_b, bout_b,
                            w_gate, w_up, w_down, out):
    x_tiles = x_in.rearrange("b (t p) e -> p (b t) e", p=P)
    out_tiles = out.rearrange("b (t p) e -> p (b t) e", p=P)
    KPARTS = 2 * PARTS - 1
    STORES = (PARTS + KPARTS) * SEM_DMA
    LOADS = 3 * PARTS * SEM_DMA
    q_parts = nc.dram_tensor("q_parts", [WINDOWS, HG, PD, S], BF16, kind="Internal").ap()
    k_parts = nc.dram_tensor("k_parts", [WINDOWS, HG, KPARTS * HD, S], BF16, kind="Internal").ap()

    with ExitStack() as ctx:
        def sb(name, shape, dt):
            return ctx.enter_context(nc.sbuf_tensor(name, shape, dt))

        def sem(name):
            return ctx.enter_context(nc.semaphore(name))

        psum = ctx.enter_context(nc.psum_tensor("psum", [P, 8, CHUNK], F32))

        x = sb("x", [P, TILES, E], F32)
        stats = sb("stats", [P, TILES, 6], F32)
        lnt = sb("lnt", [P, 6, TILES], F32)
        mean, rstd = lnt[:, 0, :], lnt[:, 1, :]
        power = sb("power", [P, TILES], F32)
        xn = sb("xn", [P, 2, TPC, E], F32)
        xt = sb("xt", [P, 2, CHUNK], F32)
        qk = sb("qk", [P, 2, 2, CHUNK], F32)
        rem = sb("rem", [P, 2, 2, CHUNK], F32)
        parts = sb("parts", [P, 2, PARTS, 2, CHUNK], BF16)
        v = sb("v", [P, WINDOWS * VW + VPAD], F32)
        vwin = sb("vwin", [P, BUFS, VW + VPAD], F32)
        qop = sb("qop", [P, BUFS, 2, HG, CHUNK], BF16)
        kop = sb("kop", [P, BUFS, HG, S], BF16)
        probs = sb("probs", [P, PROBS, 2, CHUNK], F32)
        junk = sb("junk", [P, RING, CHUNK], BF16)
        maxima = sb("maxima", [P, 2, HG, TPC, 2], F32)
        negmax = sb("negmax", [P, HG * TPC], F32)
        shift = sb("shift", [P, SHIFT_PARTS, HG * TPC], BF16)
        shift_rows = sb("shift_rows", [SHIFT_PARTS * HG * TPC, 2, P], BF16)
        sums = sb("sums", [P, 2, CHUNK], F32)
        rden = sb("rden", [P, 2, TPC * HG], F32)
        att = sb("att", [P, WINDOWS, KB, HG * HD], F32)
        ot = sb("ot", [P, 2, TPC, E], F32)
        hid = sb("hid", [P, 2, FB, CHUNK], F32)
        wqkv = sb("wqkv", [P, 2, 3, E], F32)
        wout = sb("wout", [P, 2, E], F32)
        bias_row = sb("bias_row", [1, 2, 4, E], F32)
        bqk = sb("bqk", [P, 2, 2], F32)
        bvo = sb("bvo", [P, 2, 2, E], F32)
        early = probs[:].rearrange("p u h q -> p (u h q)")
        wsize = 3 * FB * P
        wint = early[:, 0:wsize].bitcast(I32).rearrange("p (k c d) -> p k c d", k=3, c=FB)
        wflt = early[:, wsize:2 * wsize].rearrange("p (k c d) -> p k c d", k=3, c=FB)
        wqkv_raw = early[:, 2 * wsize:2 * wsize + 6 * E].rearrange("p (l n) -> p l n", l=2)
        bias_raw = early[0:1, 2 * wsize + 6 * E:2 * wsize + 12 * E].rearrange("p (l n) -> p l n", l=2)
        wffn = sb("wffn", [P, 3, FB, P], F32)
        ident = sb("ident", [P, P], F32)
        ident_bf = sb("ident_bf", [P, P], BF16)
        ones = sb("ones", [1, P], F32)
        mask = sb("mask", [P, CHUNK], F32)
        key_mask = sb("key_mask", [P, P], BF16)

        x_loaded = sem("x_loaded")
        weights_loaded = sem("weights_loaded")
        zeroed = sem("zeroed")
        consts_ready = sem("consts_ready")
        ones_ready = sem("ones_ready")
        wflt_ready = sem("wflt_ready")
        setup_psum = sem("setup_psum")
        setup_ready = sem("setup_ready")
        stats_ready = sem("stats_ready")
        dve_step = sem("dve_step")
        var_ready = sem("var_ready")
        rstd_ready = sem("rstd_ready")
        xn_ready = sem("xn_ready")
        xt_psum = sem("xt_psum")
        xt_ready = sem("xt_ready")
        qkv_psum = sem("qkv_psum")
        qk_ready = sem("qk_ready")
        rem_ready = sem("rem_ready")
        part2_ready = sem("part2_ready")
        part3_ready = sem("part3_ready")
        v_ready = sem("v_ready")
        parts_stored = [sem(f"parts_stored{p}") for p in range(2)]
        operands_loaded = [sem(f"operands_loaded{p}") for p in range(BUFS)]
        vwin_ready = sem("vwin_ready")
        ring_full = sem("ring_full")
        ring_free = sem("ring_free")
        shift_ready = sem("shift_ready")
        shift_rows_ready = sem("shift_rows_ready")
        shift_loaded = [sem(f"shift_loaded{f}") for f in range(2)]
        scores_ready = sem("scores_ready")
        probs_ready = sem("probs_ready")
        diagonals_begun = sem("diagonals_begun")
        sums_done = sem("sums_done")
        sums_ready = sem("sums_ready")
        sums_free = sem("sums_free")
        att_ready = sem("att_ready")
        ot_ready = sem("ot_ready")
        oproj_psum = sem("oproj_psum")
        otT_psum = sem("otT_psum")
        otT_ready = sem("otT_ready")
        x_mid = sem("x_mid")
        ffn_xt_psum = sem("ffn_xt_psum")
        ffn_xt_ready = sem("ffn_xt_ready")
        ffn_xn_ready = sem("ffn_xn_ready")
        gate_up_psum = sem("gate_up_psum")
        silu_ready = sem("silu_ready")
        hid_ready = sem("hid_ready")
        down_psum = sem("down_psum")
        x_new = sem("x_new")
        stored = sem("stored")

        def wait(eng, s, value):
            if isinstance(value, int) and value <= 0:
                return
            eng.wait_ge(s, value)

        def windows(eng, body, turns):
            assert turns % BUFS == 0
            with eng.Fori(0, turns // BUFS) as i:
                for p in range(BUFS):
                    body(i * BUFS + p, p)

        def chunk_loop(eng, body):
            for p in range(2):
                body(p, p)
            with eng.Fori(1, CHUNKS // 2) as i:
                for p in range(2):
                    body(i * 2 + p, p)

        block = ctx.enter_context(nc.Block())

        @block.sync
        def _(sp):
            for c in range(CHUNKS):
                sp.dma_start(x[:, c * TPC:(c + 1) * TPC, :], x_tiles[:, c * TPC:(c + 1) * TPC, :]).then_inc(x_loaded, SEM_DMA)
            for l, (w, b, wo, bo) in enumerate(((wqkv_a, bqkv_a, wout_a, bout_a), (wqkv_b, bqkv_b, wout_b, bout_b))):
                sp.dma_start(wqkv_raw[:, l, :], w).then_inc(weights_loaded, SEM_DMA)
                sp.dma_start(wout[:, l, :], wo).then_inc(weights_loaded, SEM_DMA)
                sp.dma_start(bias_raw[0:1, l, :], b.rearrange("(o n) -> o n", o=1)).then_inc(weights_loaded, SEM_DMA)
                sp.dma_start(bias_row[0:1, l, 3, :], bo.rearrange("(o n) -> o n", o=1)).then_inc(weights_loaded, SEM_DMA)
            for k, w in enumerate((w_gate, w_up)):
                sp.dma_start(wint[:, k], w.rearrange("(c p) d -> p c d", p=P)).then_inc(weights_loaded, SEM_DMA)
            sp.dma_start(wint[:, 2], w_down.rearrange("d (c p) -> d c p", p=P)).then_inc(weights_loaded, SEM_DMA)

            def store_parts(layer, i, half):
                n = layer * CHUNKS + i * 2 + half
                sp.wait_ge(qk_ready, 4 * (n + 1))
                sp.wait_ge(part2_ready, n + 1)
                sp.wait_ge(part3_ready, n + 1)
                cols = slice(half * CHUNK, (half + 1) * CHUNK)
                q_dst = q_parts.rearrange("(b g) h (i d) t -> b i (g h) d t", g=GROUPS, d=HD)
                k_dst = k_parts.rearrange("(b g) h (i d) t -> b i (g h) d t", g=GROUPS, d=HD)
                for k in range(PARTS):
                    sp.dma_start(q_dst[bass.ds(i, 1), k, :, :, cols].rearrange("o h d t -> (o h) d t"),
                                 parts[:, half, k, 0, :]).then_inc(parts_stored[half], SEM_DMA)
                for k in range(KPARTS):
                    sp.dma_start(k_dst[bass.ds(i, 1), k, :, :, cols].rearrange("o h d t -> (o h) d t"),
                                 parts[:, half, k % PARTS, 1, :]).then_inc(parts_stored[half], SEM_DMA)

            def load_operands(w, buf):
                for s in range(PARTS):
                    rows = slice(s * PD, (s + 1) * PD)
                    for f in range(2):
                        src = q_parts[bass.ds(w, 1), :, :, f * CHUNK:(f + 1) * CHUNK]
                        sp.dma_start(qop[rows, buf, f], src.rearrange("o h r t -> r (o h) t")).then_inc(operands_loaded[buf], SEM_DMA)
                    src = k_parts[bass.ds(w, 1), :, s * HD:s * HD + PD, :]
                    sp.dma_start(kop[rows, buf], src.rearrange("o h r t -> r (o h) t")).then_inc(operands_loaded[buf], SEM_DMA)

            for layer, plan in enumerate(PLANS):
                with sp.Fori(0, B) as i:
                    for half in range(2):
                        store_parts(layer, i, half)
                for p in range(2):
                    sp.wait_ge(parts_stored[p], (layer + 1) * CHUNKS // 2 * STORES)

                def shift_rows_to_operand(w, buf, f):
                    half = layer * 2 * WINDOWS + 2 * w + f
                    sp.wait_ge(shift_rows_ready, half + 1)
                    sp.dma_start(qop[SHIFT_ROW:SHIFT_ROW + SHIFT_PARTS, buf, f], shift_rows[:, f, :]).then_inc(shift_loaded[f], SEM_DMA)

                load_operands(0, 0)
                load_operands(1, 1)
                for dw, job in plan.before:
                    if job[0] == "shift":
                        shift_rows_to_operand(0, 0, job[1])

                def turn(w, buf, jobs, load):
                    if load:
                        sp.wait_ge(scores_ready, layer * WINDOWS * PLANS[0].units + w * plan.units + 1)
                        load_operands(w + 2, (buf + 2) % BUFS)
                    for dw, job in jobs:
                        if job[0] == "shift":
                            shift_rows_to_operand(w + dw, (buf + dw) % BUFS, job[1])

                windows(sp, lambda w, buf: turn(w, buf, plan.turn_jobs, True), WINDOWS - 1 - BUFS)
                for w in range(WINDOWS - 1 - BUFS, WINDOWS - 1):
                    turn(w, w % BUFS, plan.turn_jobs, w + 2 < WINDOWS)
                turn(WINDOWS - 1, (WINDOWS - 1) % BUFS, plan.last_jobs, False)

            for c in range(CHUNKS):
                sp.wait_ge(x_new, CHUNKS + c + 1)
                sp.dma_start(out_tiles[:, c * TPC:(c + 1) * TPC, :], x[:, c * TPC:(c + 1) * TPC, :]).then_inc(stored, SEM_DMA)
            sp.wait_ge(stored, CHUNKS * SEM_DMA)

        @block.gpsimd
        def _(pool):
            nc.gpsimd.memset(ident[:], 0.0).then_inc(zeroed, 1)
            nc.gpsimd.memset(mask[:], 0.0).then_inc(zeroed, 1)
            nc.gpsimd.memset(key_mask[:], 0.0)
            nc.gpsimd.memset(ones[:], 1.0)
            nc.gpsimd.memset(power[:], -0.5)
            nc.gpsimd.memset(v[:], 1.0)
            nc.gpsimd.memset(qop[:], 0.0)
            nc.gpsimd.memset(kop[:], 0.0).then_inc(zeroed, 1)
            pool.wait_ge(zeroed, 3)
            nc.gpsimd.affine_select(out=ident[:], in_=ident[:], compare_op=ALU.not_equal, fill=1.0, base=0,
                                    pattern=[[-1, P]], channel_multiplier=1).then_inc(zeroed, 1)
            nc.gpsimd.affine_select(out=mask[:, CHUNK - P:], in_=mask[:, CHUNK - P:], compare_op=ALU.is_ge, fill=MASKED, base=0,
                                    pattern=[[-1, P]], channel_multiplier=1)
            nc.gpsimd.affine_select(out=key_mask[:], in_=key_mask[:], compare_op=ALU.is_ge, fill=MASKED, base=0,
                                    pattern=[[1, P]], channel_multiplier=-1)
            pool.wait_ge(zeroed, 4)
            nc.gpsimd.tensor_copy(ident_bf[:], ident[:]).then_inc(consts_ready, 1)

            ln_count = [0]

            def inverse_deviation():
                ln_count[0] += 1
                pool.wait_ge(var_ready, ln_count[0])
                nc.gpsimd.tensor_tensor(rstd, lnt[:, 5, :], power[:], ALU.pow).then_inc(rstd_ready, 1)

            for layer, plan in enumerate(PLANS):
                inverse_deviation()

                def third_part(n, buf):
                    g = layer * CHUNKS + n
                    pool.wait_ge(part2_ready, g + 1)
                    wait(pool, parts_stored[buf], (g - buf) * (STORES // 2))
                    nc.gpsimd.tensor_tensor(parts[:, buf, 2], rem[:, buf], parts[:, buf, 1], ALU.subtract).then_inc(part3_ready, 1)

                chunk_loop(pool, third_part)

                pool.wait_ge(v_ready, (layer + 1) * CHUNKS)
                sums_base = layer * WINDOWS * PLANS[0].n

                def copy_v(w, buf):
                    nc.gpsimd.tensor_copy(vwin[:, buf, :], v[:, bass.ds(w * VW, VW + VPAD)]).then_inc(vwin_ready, 1)

                copy_v(0, 0)
                copy_v(1, 1)

                def turn(w, buf):
                    pool.wait_ge(sums_done, sums_base + w * plan.n + 1)
                    copy_v(w + 2, (buf + 2) % BUFS)

                windows(pool, turn, WINDOWS - 1 - BUFS)
                for w in range(WINDOWS - 1 - BUFS, WINDOWS - 2):
                    turn(w, w % BUFS)
                inverse_deviation()

        @block.scalar
        def _(act):
            act.wait_ge(setup_psum, 1)
            nc.scalar.copy(bqk[:].rearrange("p l t -> p (l t)"), psum[:, 0, 0:4])
            nc.scalar.copy(bvo[:].rearrange("p l t e -> p (l t e)"), psum[:, 1, :]).then_inc(setup_ready, 1)
            for k in range(3):
                act.wait_ge(setup_psum, 2 + k)
                nc.scalar.copy(wffn[:, k].rearrange("p c d -> p (c d)"), psum[:, 2 + k, 0:HIDDEN]).then_inc(setup_ready, 1)

            for layer, plan in enumerate(PLANS):
                def qkv_chunk(n, buf):
                    g = layer * CHUNKS + n
                    act.wait_ge(xt_psum, g + 1)
                    wait(act, qkv_psum, 3 * (g - 1))
                    nc.scalar.copy(xt[:, buf, :], psum[:, buf, :]).then_inc(xt_ready, 1)
                    for t in range(2):
                        act.wait_ge(qkv_psum, 3 * g + t + 1)
                        if t == 0:
                            wait(act, part3_ready, g - 1)
                            wait(act, rem_ready, g - 1)
                            wait(act, parts_stored[buf], (g - buf) * (STORES // 2))
                        src = psum[:, 2 + 3 * buf + t, :]
                        nc.scalar.activation(qk[:, buf, t, :], src, ACT.Identity, bias=bqk[:, layer, t:t + 1]).then_inc(qk_ready, 1)
                        nc.scalar.activation(parts[:, buf, 0, t, :], src, ACT.Identity, bias=bqk[:, layer, t:t + 1]).then_inc(qk_ready, 1)

                chunk_loop(act, qkv_chunk)

                units_base = layer * WINDOWS * PLANS[0].units
                sums_base = layer * WINDOWS * PLANS[0].n
                half_base = layer * 2 * WINDOWS

                def exp_units(w, wmod, s):
                    f, j, c0 = plan.steps[s]
                    for pair in range(2):
                        unit = w * plan.units + 2 * s + pair
                        slot = (wmod * plan.units + 2 * s + pair) % PROBS
                        act.wait_ge(scores_ready, units_base + unit + 1)
                        if pair == 0:
                            before = w * plan.n + s + 1 - PROBS // 2
                            if not (isinstance(before, int) and before <= 0):
                                act.wait_ge(sums_done, sums_base + before)
                        nc.scalar.activation(probs[:, slot, :, c0:], psum[:, 2 * pair:2 * pair + 2, c0:], ACT.Exp,
                                             scale=SCORE_SCALE).then_inc(probs_ready, 1)
                    if s == plan.half_end[0] + 1:
                        copy_sums(w, 0)

                def copy_sums(w, f):
                    last = w * plan.n + plan.half_end[f]
                    act.wait_ge(sums_done, sums_base + last + 1)
                    act.wait_ge(sums_free, half_base + 2 * w + f + 1)
                    nc.scalar.copy(sums[:, f, :], psum[:, 7, :]).then_inc(sums_ready, 1)

                for s in range(plan.turn):
                    exp_units(0, 0, s)

                def turn(w, buf, steps):
                    for dw, s in steps:
                        exp_units(w + dw, (buf + dw) % BUFS, s)
                        if dw == 1 and s == 0:
                            copy_sums(w, 1)

                windows(act, lambda w, buf: turn(w, buf, plan.turn_steps), WINDOWS - 1)
                turn(WINDOWS - 1, (WINDOWS - 1) % BUFS, plan.turn_steps[:plan.n - plan.turn])
                copy_sums(WINDOWS - 1, 1)

                def oproj_chunk(n, buf):
                    g = layer * CHUNKS + n
                    act.wait_ge(att_ready, half_base + 2 * WINDOWS)
                    wait(act, otT_psum, g - 1)
                    src = att[:, bass.ds((n // 2) * GROUPS, GROUPS), TPC * buf:TPC * (buf + 1), :].rearrange("p g t e -> p t g e")
                    nc.scalar.copy(ot[:, buf].rearrange("p t (g e) -> p t g e", g=GROUPS), src).then_inc(ot_ready, 1)
                    act.wait_ge(otT_psum, g + 1)
                    wait(act, oproj_psum, g - 1)
                    nc.scalar.copy(xt[:, buf, :], psum[:, buf, :]).then_inc(otT_ready, 1)

                chunk_loop(act, oproj_chunk)

                def ffn_chunk(n, buf):
                    g = layer * CHUNKS + n
                    act.wait_ge(ffn_xt_psum, g + 1)
                    wait(act, gate_up_psum, 2 * FB * (g - 1))
                    nc.scalar.copy(xt[:, buf, :], psum[:, buf, :]).then_inc(ffn_xt_ready, 1)
                    for c in range(FB):
                        act.wait_ge(gate_up_psum, 2 * FB * g + 2 * c + 1)
                        if c == 0:
                            wait(act, down_psum, g - 1)
                        nc.scalar.activation(hid[:, buf, c, :], psum[:, 2 + 2 * ((buf * FB + c) % 2), :], ACT.Silu).then_inc(silu_ready, 1)

                chunk_loop(act, ffn_chunk)

        @block.vector
        def _(dve):
            chain = [0]

            def link(ins):
                chain[0] += 1
                ins.then_inc(dve_step, 1)
                dve.wait_ge(dve_step, chain[0])

            dve.wait_ge(weights_loaded, 11 * SEM_DMA)
            for l in range(2):
                for dst, src in ((wqkv[:, l], wqkv_raw[:, l]), (bias_row[0:1, l, 0:3], bias_raw[:, l])):
                    nc.vector.tensor_copy(dst.rearrange("p t (h d) -> p t h d", d=HD),
                                          src.rearrange("p (h t d) -> p t h d", t=3, d=HD))
            nc.vector.tensor_scalar(wflt, wint, DEQUANT, None, ALU.mult).then_inc(wflt_ready, 1)

            def row_stats_all():
                for c in range(CHUNKS):
                    dve.wait_ge(x_loaded, CHUNKS * SEM_DMA)
                    for t in range(TPC):
                        ins = nc.vector.bn_stats(stats[:, c * TPC + t, :], x[:, c * TPC + t, :])
                ins.then_inc(stats_ready, 1)

            stats_count = [0]

            def mean_and_variance():
                stats_count[0] += 1
                st = stats[:].rearrange("p t s -> p s t")
                half = 0.5
                dve.wait_ge(stats_ready, stats_count[0])
                nc.vector.tensor_tensor(lnt[:, 2, :], st[:, 1], st[:, 4], ALU.add)
                nc.vector.tensor_tensor(lnt[:, 3, :], st[:, 1], st[:, 4], ALU.subtract)
                link(nc.vector.tensor_tensor(lnt[:, 4, :], st[:, 2], st[:, 5], ALU.add))
                nc.vector.tensor_scalar(mean, lnt[:, 2, :], half, None, ALU.mult)
                nc.vector.tensor_scalar(lnt[:, 4, :], lnt[:, 4, :], 1.0 / E, EPS, ALU.mult, ALU.add)
                link(nc.vector.scalar_tensor_tensor(out=lnt[:, 3, :], in0=lnt[:, 3, :], scalar=0.25, in1=lnt[:, 3, :],
                                                    op0=ALU.mult, op1=ALU.mult))
                nc.vector.tensor_tensor(lnt[:, 5, :], lnt[:, 3, :], lnt[:, 4, :], ALU.add).then_inc(var_ready, 1)
                dve.wait_ge(rstd_ready, stats_count[0])

            def normalise(n, buf, done):
                for t in range(TPC):
                    col = bass.ds(n * TPC + t, 1)
                    ins = nc.vector.tensor_scalar(xn[:, buf, t, :], x[:, col, :].rearrange("p o e -> p (o e)"), mean[:, col], rstd[:, col],
                                                  ALU.subtract, ALU.mult)
                ins.then_inc(done, 1)

            def add_to_x(n, bank, done):
                tiles = bass.ds(n * TPC, TPC)
                ins = nc.vector.tensor_tensor(x[:, tiles, :], psum[:, bank, :].rearrange("p (t e) -> p t e", e=E), x[:, tiles, :], ALU.add)
                ins.then_inc(done, 1)

            def row_stats(n, x_done, count):
                dve.wait_ge(x_done, count)
                for t in range(TPC):
                    col = bass.ds(n * TPC + t, 1)
                    ins = nc.vector.bn_stats(stats[:, col, :].rearrange("p o s -> p (o s)"), x[:, col, :].rearrange("p o e -> p (o e)"))
                return ins

            row_stats_all()
            dve.wait_ge(setup_ready, 4)
            for layer, plan in enumerate(PLANS):
                mean_and_variance()

                def qkv_chunk(n, buf):
                    g = layer * CHUNKS + n
                    wait(dve, xt_psum, g - 1)
                    normalise(n, buf, xn_ready)

                def split_chunk(n, buf):
                    g = layer * CHUNKS + n
                    dve.wait_ge(qk_ready, 4 * (g + 1))
                    wait(dve, part3_ready, g - 1)
                    nc.vector.tensor_tensor(rem[:, buf], qk[:, buf], parts[:, buf, 0], ALU.subtract).then_inc(rem_ready, 1)
                    dve.wait_ge(rem_ready, g + 1)
                    wait(dve, parts_stored[buf], (g - buf) * (STORES // 2))
                    nc.vector.tensor_copy(parts[:, buf, 1], rem[:, buf]).then_inc(part2_ready, 1)
                    dve.wait_ge(qkv_psum, 3 * (g + 1))
                    bv = bvo[:, layer, 0, :].rearrange("p (g c d) -> p g c d", g=GROUPS, d=HD)
                    for t in range(TPC):
                        kb = TPC * buf + t
                        vb = v[:, bass.ds((n // 2) * GROUPS * VW, GROUPS * VW)].rearrange("p (g k c d) -> p g k c d", g=GROUPS, k=KB, d=VH)
                        ins = nc.vector.tensor_tensor(
                            vb[:, :, kb, :, 0:HD],
                            psum[:, 4 + 3 * buf, t * P:(t + 1) * P].rearrange("p (g c d) -> p g c d", g=GROUPS, d=HD), bv, ALU.add)
                    ins.then_inc(v_ready, 1)

                if layer == 0:
                    dve.wait_ge(consts_ready, 1)
                    nc.vector.memset(kop[SHIFT_ROW:SHIFT_ROW + SHIFT_PARTS], 1.0).then_inc(ones_ready, 1)
                else:
                    dve.wait_ge(vwin_ready, layer * WINDOWS)
                qkv_chunk(0, 0)
                for p in range(2):
                    qkv_chunk(p + 1, (p + 1) % 2)
                    split_chunk(p, p)
                with dve.Fori(1, CHUNKS // 2 - 1) as i:
                    for p in range(2):
                        qkv_chunk(i * 2 + p + 1, (p + 1) % 2)
                        split_chunk(i * 2 + p, p)
                qkv_chunk(CHUNKS - 1, 1)
                split_chunk(CHUNKS - 2, 0)
                split_chunk(CHUNKS - 1, 1)

                job_base = layer * PLANS[0].jobs_all
                half_base = layer * 2 * WINDOWS
                if layer == 0:
                    dve.sem_inc(sums_free, 2)

                def make_shift(w, f, last_max):
                    kh = maxima[:, f, :, :, 0:1] if plan.causal and f == 0 else maxima[:, f]
                    dve.wait_ge(ring_free, last_max + 1)
                    nc.vector.tensor_reduce(negmax[:].rearrange("p (h t) -> p h t", h=HG), kh, AX_X, ALU.max, negate=True).then_inc(shift_ready, 1)
                    half = half_base + 2 * w + f
                    dve.wait_ge(shift_ready, 3 * half + 1)
                    nc.vector.tensor_copy(shift[:, 0, :], negmax[:]).then_inc(shift_ready, 1)
                    dve.wait_ge(shift_ready, 3 * half + 2)
                    nc.vector.tensor_tensor(shift[:, 1, :], negmax[:], shift[:, 0, :], ALU.subtract).then_inc(shift_ready, 1)

                def run_job(w, job, index, static_index):
                    slot = 4 + static_index % RING
                    dve.wait_ge(ring_full, index + 1)
                    if job[0] == "max":
                        _, f, c, qb, kh, width, diagonal = job
                        dst = maxima[:, f, c, qb, kh:kh + 1]
                        if diagonal:
                            dve.sem_inc(diagonals_begun, 1)
                            nc.vector.tensor_tensor_reduce(out=junk[:, slot - 4, 0:width], in0=psum[:, slot, 0:width], in1=mask[:, CHUNK - width:],
                                                           scale=1.0, scalar=LOWEST, op0=ALU.add, op1=ALU.max, accum_out=dst).then_inc(ring_free, 1)
                        else:
                            nc.vector.tensor_reduce(dst, psum[:, slot, 0:width], AX_X, ALU.max).then_inc(ring_free, 1)
                        if (c, qb, kh) == (HG - 1, TPC - 1, 0 if plan.causal and f == 0 else 1):
                            make_shift(w, f, index)
                    elif job[0] == "shift":
                        f = job[1]
                        rows = SHIFT_PARTS * HG * TPC
                        nc.vector.tensor_copy(shift_rows[:, f, :], psum[0:rows, slot, 0:P // 2].bitcast(BF16)).then_inc(ring_free, 1)
                        dve.wait_ge(ring_free, index + 1)
                        dve.sem_inc(shift_rows_ready, 1)
                    else:
                        f = job[1]
                        t = psum[:, slot, :].rearrange("p (t h m) -> p t h m", t=TPC, h=HG)
                        half = half_base + 2 * w + f
                        nc.vector.reciprocal(rden[:, f, :].rearrange("p (t h) -> p t h", h=HG), t[:, :, :, HD]).then_inc(att_ready, 1)
                        dve.wait_ge(att_ready, 2 * half + 1)
                        nc.vector.tensor_tensor(
                            att[:, bass.ds(w, 1), TPC * f:TPC * (f + 1), :].rearrange("p o t (h d) -> p (o t) h d", h=HG), t[:, :, :, 0:HD],
                            rden[:, f, :].rearrange("p (t h o) -> p t h o", h=HG, o=1).broadcast_to([P, TPC, HG, HD]), ALU.mult)\
                            .then_inc(att_ready, 1)
                        dve.wait_ge(att_ready, 2 * half + 2)
                        dve.sem_inc(ring_free, 1)
                        dve.sem_inc(sums_free, 1)

                def run_jobs(w, placed, index, static_index):
                    for step in placed:
                        for slot in step:
                            for dw, job in slot:
                                run_job(w + dw, job, index, static_index)
                                index = index + 1
                                static_index += 1

                for k, (dw, job) in enumerate(plan.before):
                    run_job(0, job, job_base + k, job_base + k)
                first = job_base + plan.jobs_before
                windows(dve, lambda w, buf: run_jobs(w, plan.turn_plan, w * plan.jobs_turn + first, buf * plan.jobs_turn + first), WINDOWS - 1)
                run_jobs(WINDOWS - 1, plan.last_plan + [[[(0, ("norm", 1))]]], (WINDOWS - 1) * plan.jobs_turn + first,
                         (WINDOWS - 1) * plan.jobs_turn + first)

                def oproj_chunk(n, buf):
                    g = layer * CHUNKS + n
                    tiles = bass.ds(n * TPC, TPC)
                    bo = bvo[:, layer, 1:2, :].broadcast_to([P, TPC, E])
                    nc.vector.tensor_tensor(x[:, tiles, :], x[:, tiles, :], bo, ALU.add).then_inc(x_mid, 1)
                    dve.wait_ge(oproj_psum, g + 1)
                    dve.wait_ge(x_mid, 2 * g + 1)
                    add_to_x(n, 2 + buf, x_mid)
                    return row_stats(n, x_mid, 2 * g + 2)

                chunk_loop(dve, oproj_chunk)
                link(nc.vector.memset(junk[:, 0, 0:2], 0.0))
                dve.sem_inc(stats_ready, 1)
                mean_and_variance()

                def ffn_normalise(n, buf):
                    wait(dve, ffn_xt_psum, layer * CHUNKS + n - 1)
                    normalise(n, buf, ffn_xn_ready)

                def ffn_gate(n, buf):
                    g = layer * CHUNKS + n
                    for c in range(FB):
                        dve.wait_ge(silu_ready, FB * g + c + 1)
                        dve.wait_ge(gate_up_psum, 2 * FB * g + 2 * c + 2)
                        nc.vector.tensor_tensor(hid[:, buf, c, :], psum[:, 3 + 2 * ((buf * FB + c) % 2), :], hid[:, buf, c, :], ALU.mult).then_inc(hid_ready, 1)

                def ffn_residual(n, buf):
                    g = layer * CHUNKS + n
                    dve.wait_ge(down_psum, g + 1)
                    add_to_x(n, 6 + buf, x_new)
                    if layer == 0:
                        row_stats(n, x_new, g + 1)

                ffn_normalise(0, 0)
                ffn_normalise(1, 1)
                ffn_gate(0, 0)
                for p in range(1, 3):
                    ffn_normalise(p + 1, (p + 1) % 2)
                    ffn_gate(p, p % 2)
                    ffn_residual(p - 1, (p - 1) % 2)
                with dve.Fori(1, CHUNKS // 2 - 1) as i:
                    for p in range(1, 3):
                        ffn_normalise(i * 2 + p + 1, (p + 1) % 2)
                        ffn_gate(i * 2 + p, p % 2)
                        ffn_residual(i * 2 + p - 1, (p - 1) % 2)
                ffn_gate(CHUNKS - 1, 1)
                ffn_residual(CHUNKS - 2, 0)
                ffn_residual(CHUNKS - 1, 1)
                if layer == 0:
                    link(nc.vector.memset(junk[:, 0, 0:2], 0.0))
                    dve.sem_inc(stats_ready, 1)

        @block.tensor
        def _(pe):
            mm = nc.tensor.matmul
            pe.wait_ge(weights_loaded, 11 * SEM_DMA)
            pe.wait_ge(wflt_ready, 1)
            pe.wait_ge(consts_ready, 1)
            for l in range(2):
                for t in range(2):
                    mm(psum[:, 0, 2 * l + t:2 * l + t + 1], bias_row[0:1, l, t, :], ones[0:1, 0:1], start=True, stop=True)
            for l in range(2):
                mm(psum[:, 1, 2 * l * E:2 * l * E + E], ones[0:1, :], bias_row[0:1, l, 2, :], start=True, stop=True)
                ins = mm(psum[:, 1, 2 * l * E + E:2 * l * E + 2 * E], ones[0:1, :], bias_row[0:1, l, 3, :], start=True, stop=True)
            ins.then_inc(setup_psum, 1)
            for k in range(3):
                for c in range(FB):
                    ins = nc.tensor.transpose(psum[:, 2 + k, c * P:(c + 1) * P], wflt[:, k, c, :], ident[:])
                ins.then_inc(setup_psum, 1)
            pe.wait_ge(setup_ready, 4)

            def transpose_chunk(src, buf, done):
                for t in range(TPC):
                    ins = nc.tensor.transpose(psum[:, buf, t * P:(t + 1) * P], src[:, buf, t, :], ident[:])
                ins.then_inc(done, 1)

            for layer, plan in enumerate(PLANS):
                def xn_transpose(n, buf):
                    g = layer * CHUNKS + n
                    pe.wait_ge(xn_ready, g + 1)
                    wait(pe, xt_ready, g - 1)
                    transpose_chunk(xn, buf, xt_psum)

                def qkv_products(n, buf):
                    g = layer * CHUNKS + n
                    pe.wait_ge(xt_ready, g + 1)
                    for t in range(2):
                        if t == 0:
                            wait(pe, qk_ready, 4 * (g - 1))
                        mm(psum[:, 2 + 3 * buf + t, :], wqkv[:, layer, t, :], xt[:, buf, :], start=True, stop=True).then_inc(qkv_psum, 1)
                    wait(pe, v_ready, g - 1)
                    for t in range(TPC):
                        ins = mm(psum[:, 4 + 3 * buf, t * P:(t + 1) * P], xt[:, buf, t * P:(t + 1) * P], wqkv[:, layer, 2, :],
                                 start=True, stop=True)
                    ins.then_inc(qkv_psum, 1)

                xn_transpose(0, 0)
                for p in range(2):
                    xn_transpose(p + 1, (p + 1) % 2)
                    qkv_products(p, p)
                with pe.Fori(1, CHUNKS // 2 - 1) as i:
                    for p in range(2):
                        xn_transpose(i * 2 + p + 1, (p + 1) % 2)
                        qkv_products(i * 2 + p, p)
                xn_transpose(CHUNKS - 1, 1)
                qkv_products(CHUNKS - 2, 0)
                qkv_products(CHUNKS - 1, 1)
                pe.wait_ge(ones_ready, 1)
                pe.wait_ge(qk_ready, 4 * (layer + 1) * CHUNKS)
                pe.wait_ge(v_ready, (layer + 1) * CHUNKS)

                job_base = layer * PLANS[0].jobs_all
                units_base = layer * WINDOWS * PLANS[0].units
                sums_base = layer * WINDOWS * PLANS[0].n
                half_base = layer * 2 * WINDOWS
                diagonal_steps = [s for s, (f, j, c0) in enumerate(plan.steps) if plan.causal and j * P >= f * CHUNK]

                def run_job(w, buf, job, index, static_index, first):
                    slot = 4 + static_index % RING
                    if static_index - job_base >= RING or not first:
                        pe.wait_ge(ring_free, index - RING + 1)
                    if job[0] == "max":
                        _, f, c, qb, kh, width, _ = job
                        if (f, c, qb, kh) == (0, 0, 0, 0):
                            earlier = layer * len(range(buf, WINDOWS, BUFS))
                            pe.wait_ge(operands_loaded[buf], (w - buf) * (LOADS // BUFS) + (earlier + 1) * LOADS)
                        mm(psum[:, slot, 0:width], qop[0:SHIFT_ROW, buf, f, c, qb * P:(qb + 1) * P], kop[0:SHIFT_ROW, buf, c, kh * CHUNK:kh * CHUNK + width],
                           start=True, stop=True).then_inc(ring_full, 1)
                    elif job[0] == "shift":
                        half = half_base + 2 * w + job[1]
                        pe.wait_ge(shift_ready, 3 * (half + 1))
                        nc.tensor.transpose(psum[0:SHIFT_PARTS * HG * TPC, slot, 0:P // 2].bitcast(BF16),
                                            shift[:].rearrange("p k n -> p (k n)"), ident_bf[:]).then_inc(ring_full, 1)
                    else:
                        f = job[1]
                        half = half_base + 2 * w + f
                        pe.wait_ge(sums_ready, half + 1)
                        for t in range(TPC):
                            ins = nc.tensor.transpose(psum[:, slot, t * P:(t + 1) * P], sums[:, f, t * P:(t + 1) * P], ident[:])
                        ins.then_inc(ring_full, 1)

                def scores(w, buf, s, pair):
                    f, j, c0 = plan.steps[s]
                    if s == plan.half_start[f] and pair == 0:
                        pe.wait_ge(shift_loaded[f], (layer * WINDOWS + w + 1) * SEM_DMA)
                    before = w * plan.units + 2 * s + pair - 1
                    if not (isinstance(before, int) and before <= 0):
                        pe.wait_ge(probs_ready, units_base + before)
                    for h in range(2):
                        c = 2 * pair + h
                        ins = mm(psum[:, c, c0:], kop[:, buf, c, j * P:(j + 1) * P], qop[:, buf, f, c, c0:],
                                 start=True, stop=s not in diagonal_steps)
                        if s in diagonal_steps:
                            ins = mm(psum[:, c, c0:c0 + P], ident_bf[:], key_mask[:], start=False, stop=True)
                    ins.then_inc(scores_ready, 1)

                def weighted_sums(w, buf, s):
                    f, j, c0 = plan.steps[s]
                    if s == 0:
                        pe.wait_ge(vwin_ready, layer * WINDOWS + w + 1)
                    if s == plan.half_start[f]:
                        wait(pe, sums_ready, half_base + 2 * w + f)
                    pe.wait_ge(probs_ready, units_base + w * plan.units + 2 * s + 2)
                    for c in range(HG):
                        slot = (buf * plan.units + 2 * s + c // 2) % PROBS
                        at = (j * HG + c) * VH
                        ins = mm(psum[32 * c:32 * c + 32, 7, c0:], vwin[:, buf, at:at + 32], probs[:, slot, c % 2, c0:],
                                 start=(j == 0), stop=(s == plan.half_end[f]), tile_position=(0, 32 * c))
                    ins.then_inc(sums_done, 1)

                def step(w, buf, dw, s, slots, index, static_index, prev):
                    for part in range(4):
                        for jw, job in slots[part]:
                            run_job(w + jw, (buf + jw) % BUFS, job, index, static_index, False)
                            index = index + 1
                            static_index += 1
                        if part < 2:
                            scores(w + dw, (buf + dw) % BUFS, s, part)
                        elif part == 2 and prev is not None:
                            weighted_sums(w + prev[0], (buf + prev[0]) % BUFS, prev[1])
                    return index, static_index

                def turn(w, buf, steps, placed, index, static_index):
                    prev = (0, plan.turn - 1)
                    for (dw, s), slots in zip(steps, placed):
                        index, static_index = step(w, buf, dw, s, slots, index, static_index, prev)
                        prev = (dw, s)
                    return index, static_index

                for k, (dw, job) in enumerate(plan.before):
                    run_job(0, 0, job, job_base + k, job_base + k, True)
                first = job_base + plan.jobs_before
                for s in range(plan.turn):
                    scores(0, 0, s, 0)
                    scores(0, 0, s, 1)
                    if s:
                        weighted_sums(0, 0, s - 1)
                windows(pe, lambda w, buf: turn(w, buf, plan.turn_steps, plan.turn_plan, w * plan.jobs_turn + first,
                                                buf * plan.jobs_turn + first), WINDOWS - 1)
                last, last_buf = WINDOWS - 1, (WINDOWS - 1) % BUFS
                index, _ = turn(last, last_buf, plan.turn_steps[:plan.n - plan.turn], plan.last_plan, last * plan.jobs_turn + first,
                                last * plan.jobs_turn + first)
                weighted_sums(last, last_buf, plan.n - 1)
                run_job(last, last_buf, ("norm", 1), index, index, False)
                pe.wait_ge(ring_free, job_base + plan.jobs_all)

                def oproj_transpose(n, buf):
                    g = layer * CHUNKS + n
                    pe.wait_ge(ot_ready, g + 1)
                    wait(pe, otT_ready, g - 1)
                    transpose_chunk(ot, buf, otT_psum)

                def oproj_products(n, buf):
                    g = layer * CHUNKS + n
                    pe.wait_ge(otT_ready, g + 1)
                    wait(pe, x_mid, 2 * (g - 1))
                    for t in range(TPC):
                        ins = mm(psum[:, 2 + buf, t * P:(t + 1) * P], xt[:, buf, t * P:(t + 1) * P], wout[:, layer, :], start=True, stop=True)
                    ins.then_inc(oproj_psum, 1)

                oproj_transpose(0, 0)
                for p in range(2):
                    oproj_transpose(p + 1, (p + 1) % 2)
                    oproj_products(p, p)
                with pe.Fori(1, CHUNKS // 2 - 1) as i:
                    for p in range(2):
                        oproj_transpose(i * 2 + p + 1, (p + 1) % 2)
                        oproj_products(i * 2 + p, p)
                oproj_transpose(CHUNKS - 1, 1)
                oproj_products(CHUNKS - 2, 0)
                oproj_products(CHUNKS - 1, 1)
                pe.wait_ge(x_mid, 2 * (layer + 1) * CHUNKS)

                def ffn_transpose(n, buf):
                    g = layer * CHUNKS + n
                    pe.wait_ge(ffn_xn_ready, g + 1)
                    wait(pe, ffn_xt_ready, g - 1)
                    transpose_chunk(xn, buf, ffn_xt_psum)

                def ffn_gate_up(n, buf):
                    g = layer * CHUNKS + n
                    pe.wait_ge(ffn_xt_ready, g + 1)
                    for c in range(FB):
                        wait(pe, hid_ready, FB * g + c - 1)
                        for k in range(2):
                            mm(psum[:, 2 + 2 * ((buf * FB + c) % 2) + k, :], wffn[:, k, c, :], xt[:, buf, :], start=True, stop=True).then_inc(gate_up_psum, 1)

                def ffn_down(n, buf):
                    g = layer * CHUNKS + n
                    pe.wait_ge(hid_ready, FB * (g + 1))
                    wait(pe, x_new, g - 1)
                    for t in range(TPC):
                        for c in range(FB):
                            ins = mm(psum[:, 6 + buf, t * P:(t + 1) * P], hid[:, buf, c, t * P:(t + 1) * P], wffn[:, 2, c, :],
                                     start=(c == 0), stop=(c == FB - 1))
                    ins.then_inc(down_psum, 1)

                ffn_transpose(0, 0)
                ffn_transpose(1, 1)
                ffn_gate_up(0, 0)
                for p in range(1, 3):
                    ffn_transpose(p + 1, (p + 1) % 2)
                    ffn_gate_up(p, p % 2)
                    ffn_down(p - 1, (p - 1) % 2)
                with pe.Fori(1, CHUNKS // 2 - 1) as i:
                    for p in range(1, 3):
                        ffn_transpose(i * 2 + p + 1, (p + 1) % 2)
                        ffn_gate_up(i * 2 + p, p % 2)
                        ffn_down(i * 2 + p - 1, (p - 1) % 2)
                ffn_gate_up(CHUNKS - 1, 1)
                ffn_down(CHUNKS - 2, 0)
                ffn_down(CHUNKS - 1, 1)
                pe.wait_ge(x_new, (layer + 1) * CHUNKS)


_INS = ["L0_attn_a_x", "L0_attn_a_Wqkv", "L0_attn_a_bqkv", "L0_attn_a_Wout", "L0_attn_a_bout",
        "L0_attn_b_W_qkv", "L0_attn_b_b_qkv", "L0_attn_b_W_out", "L0_attn_b_b_out",
        "L0_ffn_w_gate", "L0_ffn_w_up", "L0_ffn_w_down"]


def kernel(**inputs):
    import numpy as np
    import concourse.bacc as bacc
    from concourse.bass_utils import run_bass_kernel_spmd

    nc = bacc.Bacc("TRN2", target_bir_lowering=False, num_devices=1)
    arrays, args = {}, []
    for name in _INS:
        a = np.ascontiguousarray(inputs[name])
        arrays[f"in_{name}"] = a
        args.append(nc.dram_tensor(f"in_{name}", a.shape, mybir.dt.from_np(a.dtype), kind="ExternalInput").ap())
    out = nc.dram_tensor("out_x", (B, S, E), F32, kind="ExternalOutput").ap()
    transformer_pair_kernel(nc, *args, out)
    r = run_bass_kernel_spmd(nc, [arrays], core_ids=[0])
    return r.results[0]["out_x"]
```

```python
from contextlib import ExitStack

import concourse.bass as bass
from concourse import mybir
from concourse.alu_op_type import AluOpType as ALU

ACT = mybir.ActivationFunctionType
F32 = mybir.dt.float32
BF16 = mybir.dt.bfloat16
I32 = mybir.dt.int32
AX_X = mybir.AxisListType.X

P = 128
B, S, E, H = 4, 1024, 128, 16
HD = E // H
HIDDEN = 384
FB = HIDDEN // P
EPS = 1e-5
DEQUANT = 1.0 / 127.0
SCORE_SCALE = float(HD) ** -0.5
MASKED = -1.0e30
LOWEST = -3.0e38

TILES = B * S // P
CHUNK = 512
TPC = CHUNK // P
CHUNKS = B * S // CHUNK
KB = S // P
HG = 4
GROUPS = H // HG
WINDOWS = B * GROUPS
PARTS = 3
PD = PARTS * HD
TERMS = PARTS * PD
SHIFT_ROW = 96
SHIFT_PARTS = 2
VH = HD + 1
VW = KB * HG * VH
VPAD = 32 - VH
BUFS = 3
RING = 3
PROBS = 6
SEM_DMA = 16


class Plan:

    def __init__(self, causal, turn, cut, idle_steps):
        self.causal = causal
        self.turn = turn
        self.steps = []
        for f in range(2):
            for j in range(KB):
                c0 = max(0, j * P - f * CHUNK) if causal else 0
                if c0 < CHUNK:
                    self.steps.append((f, j, c0))
        n = self.n = len(self.steps)
        self.half_start = [0, sum(1 for s in self.steps if s[0] == 0)]
        self.half_end = [self.half_start[1] - 1, n - 1]
        stream = []
        for f in range(2):
            for qb in range(TPC):
                for c in range(HG):
                    width = (TPC * f + qb + 1) * P if causal else S
                    for kh in range(2):
                        w = min(width - kh * CHUNK, CHUNK)
                        if w > 0:
                            stream.append((f, c, qb, kh, w, causal and kh * CHUNK + w == width))
        cut = len(stream) if cut is None else cut
        self.before = [(0, x) for x in stream[:cut]]
        jobs = [(0, x) for x in stream[cut:]] + [(1, x) for x in stream[:cut]]
        self.turn_steps = [(0, s) for s in range(turn, n)] + [(1, s) for s in range(turn)]
        slots = [0 if i >= n - idle_steps else CHUNK - self.steps[s][2] for i, (_, s) in enumerate(self.turn_steps) for _ in range(4)]
        total_c, total_s = sum(x[4] for _, x in jobs), sum(slots)
        placed, k, done_c, done_s = [], 0, 0, 0
        for w in slots:
            done_s += w
            slot = []
            while k < len(jobs) and (done_c + jobs[k][1][4] / 2) * total_s <= done_s * total_c:
                slot.append(jobs[k])
                done_c += jobs[k][1][4]
                k += 1
            placed.append(slot)
        assert k == len(jobs)
        self.turn_jobs = [placed[4 * i: 4 * i + 4] for i in range(n)]
        self.turn_ends = [[] for _ in range(n)]
        for i, (dw, s) in enumerate(self.turn_steps):
            if (dw, s) == (0, self.half_end[0] + 2):
                self.turn_ends[i].append((0, "norm", 0))
            if (dw, s) == (1, 1):
                self.turn_ends[i].append((0, "norm", 1))
            for jw, x in (y for slot in self.turn_jobs[i] for y in slot):
                if self.ends_half(x):
                    self.turn_ends[i + 1].append((jw, "shift", x[0]))
        ends = [k for k, (_, x) in enumerate(self.before) if self.ends_half(x)]
        self.before_shifts = {min(k + 4, len(self.before) - 1): self.before[k][1][0] for k in ends}
        own = [i for i, (dw, _) in enumerate(self.turn_steps) if dw == 0]
        self.last_jobs = [[[x for x in slot if x[0] == 0] for slot in self.turn_jobs[i]] for i in own]
        self.last_ends = [[x for x in self.turn_ends[i] if x[0] == 0] for i in own]
        self.units_before = len(self.before_shifts) + 2 * turn
        self.units_turn = 2 * n + sum(map(len, self.turn_ends))
        self.units_all = (self.units_before + (WINDOWS - 1) * self.units_turn + 2 * len(own)
                          + sum(map(len, self.last_ends)) + 1)
        self.jobs_before, self.jobs_turn = len(self.before), len(jobs)
        self.jobs_all = WINDOWS * len(stream)
        assert self.units_turn % 2 == 0

    def ends_half(self, job):
        f, c, qb, kh, _, _ = job
        return (c, qb, kh) == (HG - 1, TPC - 1, 0 if self.causal and f == 0 else 1)


PLANS = [Plan(causal=False, turn=3, cut=32 + 22, idle_steps=0), Plan(causal=True, turn=2, cut=None, idle_steps=1)]


def transformer_pair_kernel(nc, x_in, wqkv_a, bqkv_a, wout_a, bout_a, wqkv_b, bqkv_b, wout_b, bout_b,
                            w_gate, w_up, w_down, out):
    x_tiles = x_in.rearrange("b (t p) e -> p (b t) e", p=P)
    out_tiles = out.rearrange("b (t p) e -> p (b t) e", p=P)
    KPARTS = 2 * PARTS - 1
    STORES = (PARTS + KPARTS) * SEM_DMA
    LOADS = 3 * PARTS * SEM_DMA
    q_parts = nc.dram_tensor("q_parts", [WINDOWS, HG, PD, S], BF16, kind="Internal").ap()
    k_parts = nc.dram_tensor("k_parts", [WINDOWS, HG, KPARTS * HD, S], BF16, kind="Internal").ap()

    with ExitStack() as ctx:
        def sb(name, shape, dt):
            return ctx.enter_context(nc.sbuf_tensor(name, shape, dt))

        def sem(name):
            return ctx.enter_context(nc.semaphore(name))

        psum = ctx.enter_context(nc.psum_tensor("psum", [P, 8, CHUNK], F32))

        x = sb("x", [P, TILES, E], F32)
        stats = sb("stats", [P, 3, TPC, 6], F32)
        moments = sb("moments", [P, 3, 6, TPC], F32)
        power = sb("power", [P, TPC], F32)
        xn = sb("xn", [P, 2, TPC, E], F32)
        xt = sb("xt", [P, 2, CHUNK], F32)
        ffn_xn = sb("ffn_xn", [P, TPC, E], F32)
        ffn_xt = sb("ffn_xt", [P, CHUNK], F32)
        qk = sb("qk", [P, 2, 2, CHUNK], F32)
        rem = sb("rem", [P, 2, 2, CHUNK], F32)
        parts = sb("parts", [P, 2, PARTS, 2, CHUNK], BF16)
        v = sb("v", [P, WINDOWS * VW + VPAD], F32)
        vwin = sb("vwin", [P, BUFS, VW + VPAD], F32)
        qop = sb("qop", [P, BUFS, 2, HG, CHUNK], BF16)
        kop = sb("kop", [P, BUFS, HG, S], BF16)
        probs = sb("probs", [P, PROBS, 2, CHUNK], F32)
        junk = sb("junk", [P, RING, CHUNK], BF16)
        maxima = sb("maxima", [P, 2, HG, TPC, 2], F32)
        negmax = sb("negmax", [P, 2, HG * TPC], F32)
        zeros = sb("zeros", [P, HG * TPC], F32)
        shift = sb("shift", [P, 2, SHIFT_PARTS, HG * TPC], BF16)
        shift_rows = sb("shift_rows", [SHIFT_PARTS * HG * TPC, 2, P], BF16)
        sums = sb("sums", [P, 2, CHUNK], F32)
        att_raw = sb("att_raw", [P, 2, TPC, HG, VH], F32)
        rden = sb("rden", [P, 2, TPC, HG], F32)
        att = sb("att", [P, WINDOWS, KB, HG * HD], F32)
        ot = sb("ot", [P, TPC, E], F32)
        ot_t = sb("ot_t", [P, CHUNK], F32)
        hid = sb("hid", [P, FB, CHUNK], F32)
        wqkv = sb("wqkv", [P, 2, 3, E], F32)
        wout = sb("wout", [P, 2, E], F32)
        bias_row = sb("bias_row", [1, 2, 4, E], F32)
        bqk = sb("bqk", [P, 2, 2], F32)
        bvo = sb("bvo", [P, 2, 2, E], F32)
        early = probs[:].rearrange("p u h q -> p (u h q)")
        wsize = 3 * FB * P
        wint = early[:, 0:wsize].bitcast(I32).rearrange("p (k c d) -> p k c d", k=3, c=FB)
        wflt = early[:, wsize:2 * wsize].rearrange("p (k c d) -> p k c d", k=3, c=FB)
        wqkv_raw = early[:, 2 * wsize:2 * wsize + 6 * E].rearrange("p (l n) -> p l n", l=2)
        bias_raw = early[0:1, 2 * wsize + 6 * E:2 * wsize + 12 * E].rearrange("p (l n) -> p l n", l=2)
        wffn = sb("wffn", [P, 3, FB, P], F32)
        ident = sb("ident", [P, P], F32)
        ident_bf = sb("ident_bf", [P, P], BF16)
        ones = sb("ones", [1, P], F32)
        mask = sb("mask", [P, CHUNK], F32)
        key_mask = sb("key_mask", [P, P], BF16)

        x_loaded = sem("x_loaded")
        weights_loaded = sem("weights_loaded")
        zeroed = sem("zeroed")
        consts_ready = sem("consts_ready")
        operands_zeroed = sem("operands_zeroed")
        ones_ready = sem("ones_ready")
        wflt_ready = sem("wflt_ready")
        setup_psum = sem("setup_psum")
        setup_ready = sem("setup_ready")
        moment_steps = [sem(f"moment_steps{k}") for k in range(2)]
        var_ready = [sem(f"var_ready{k}") for k in range(2)]
        rstd_ready = [sem(f"rstd_ready{k}") for k in range(2)]
        xn_ready = [sem(f"xn_ready{k}") for k in range(2)]
        xt_psum = [sem(f"xt_psum{k}") for k in range(2)]
        xt_ready = [sem(f"xt_ready{k}") for k in range(2)]
        qkv_psum = sem("qkv_psum")
        qk_ready = sem("qk_ready")
        rem_ready = sem("rem_ready")
        part2_ready = sem("part2_ready")
        part3_ready = sem("part3_ready")
        v_ready = sem("v_ready")
        parts_stored = [sem(f"parts_stored{p}") for p in range(2)]
        operands_loaded = [sem(f"operands_loaded{p}") for p in range(BUFS)]
        vwin_ready = sem("vwin_ready")
        x_biased = sem("x_biased")
        ring_full = sem("ring_full")
        ring_free = sem("ring_free")
        begun = sem("begun")
        negmax_ready = sem("negmax_ready")
        shift_begun = sem("shift_begun")
        shift_ready = sem("shift_ready")
        shift_loaded = [sem(f"shift_loaded{f}") for f in range(2)]
        scores_ready = sem("scores_ready")
        probs_ready = sem("probs_ready")
        sums_done = sem("sums_done")
        sums_ready = sem("sums_ready")
        rden_ready = sem("rden_ready")
        att_ready = sem("att_ready")
        ot_ready = sem("ot_ready")
        ot_psum = sem("ot_psum")
        ot_t_ready = sem("ot_t_ready")
        oproj_psum = sem("oproj_psum")
        x_mid = sem("x_mid")
        gate_up_psum = sem("gate_up_psum")
        silu_ready = sem("silu_ready")
        hid_ready = sem("hid_ready")
        down_psum = sem("down_psum")
        x_new = sem("x_new")
        stored = sem("stored")

        def wait(eng, s, value):
            if isinstance(value, int) and value <= 0:
                return
            eng.wait_ge(s, value)

        def windows(eng, body, turns):
            assert turns % BUFS == 0
            with eng.Fori(0, turns // BUFS) as i:
                for p in range(BUFS):
                    body(i * BUFS + p, p)

        def pipeline(eng, body, first=0):
            for n in range(first, 2):
                body(n, n % 2, n)
            with eng.Fori(1, CHUNKS // 2 - 1) as i:
                for p in range(2):
                    body(i * 2 + p, p, 2)
            for n in range(CHUNKS - 2, CHUNKS):
                body(n, n % 2, n)

        def stages(layer, m):
            return m + 2 < CHUNKS, 0 <= m + 1 < CHUNKS, m >= 0, m >= 0 and layer == 0

        block = ctx.enter_context(nc.Block())

        @block.sync
        def _(sp):
            for c in range(CHUNKS):
                sp.dma_start(x[:, c * TPC:(c + 1) * TPC, :], x_tiles[:, c * TPC:(c + 1) * TPC, :]).then_inc(x_loaded, SEM_DMA)
            for l, (w, b, wo, bo) in enumerate(((wqkv_a, bqkv_a, wout_a, bout_a), (wqkv_b, bqkv_b, wout_b, bout_b))):
                sp.dma_start(wqkv_raw[:, l, :], w).then_inc(weights_loaded, SEM_DMA)
                sp.dma_start(wout[:, l, :], wo).then_inc(weights_loaded, SEM_DMA)
                sp.dma_start(bias_raw[0:1, l, :], b.rearrange("(o n) -> o n", o=1)).then_inc(weights_loaded, SEM_DMA)
                sp.dma_start(bias_row[0:1, l, 3, :], bo.rearrange("(o n) -> o n", o=1)).then_inc(weights_loaded, SEM_DMA)
            for k, w in enumerate((w_gate, w_up)):
                sp.dma_start(wint[:, k], w.rearrange("(c p) d -> p c d", p=P)).then_inc(weights_loaded, SEM_DMA)
            sp.dma_start(wint[:, 2], w_down.rearrange("d (c p) -> d c p", p=P)).then_inc(weights_loaded, SEM_DMA)

            def store_parts(layer, i, half):
                n = layer * CHUNKS + i * 2 + half
                sp.wait_ge(qk_ready, 4 * (n + 1))
                sp.wait_ge(part2_ready, n + 1)
                sp.wait_ge(part3_ready, n + 1)
                cols = slice(half * CHUNK, (half + 1) * CHUNK)
                q_dst = q_parts.rearrange("(b g) h (i d) t -> b i (g h) d t", g=GROUPS, d=HD)
                k_dst = k_parts.rearrange("(b g) h (i d) t -> b i (g h) d t", g=GROUPS, d=HD)
                for k in range(PARTS):
                    sp.dma_start(q_dst[bass.ds(i, 1), k, :, :, cols].rearrange("o h d t -> (o h) d t"),
                                 parts[:, half, k, 0, :]).then_inc(parts_stored[half], SEM_DMA)
                for k in range(KPARTS):
                    sp.dma_start(k_dst[bass.ds(i, 1), k, :, :, cols].rearrange("o h d t -> (o h) d t"),
                                 parts[:, half, k % PARTS, 1, :]).then_inc(parts_stored[half], SEM_DMA)

            def load_operands(w, buf):
                for s in range(PARTS):
                    rows = slice(s * PD, (s + 1) * PD)
                    for f in range(2):
                        src = q_parts[bass.ds(w, 1), :, :, f * CHUNK:(f + 1) * CHUNK]
                        sp.dma_start(qop[rows, buf, f], src.rearrange("o h r t -> r (o h) t")).then_inc(operands_loaded[buf], SEM_DMA)
                    src = k_parts[bass.ds(w, 1), :, s * HD:s * HD + PD, :]
                    sp.dma_start(kop[rows, buf], src.rearrange("o h r t -> r (o h) t")).then_inc(operands_loaded[buf], SEM_DMA)

            for layer, plan in enumerate(PLANS):
                with sp.Fori(0, B) as i:
                    for half in range(2):
                        store_parts(layer, i, half)
                for p in range(2):
                    sp.wait_ge(parts_stored[p], (layer + 1) * CHUNKS // 2 * STORES)
                unit_base = layer * PLANS[0].units_all
                if layer == 0:
                    sp.wait_ge(ones_ready, 3)

                def shift_to_operand(f, buf, unit):
                    sp.wait_ge(probs_ready, unit + 1)
                    sp.dma_start(qop[SHIFT_ROW:SHIFT_ROW + SHIFT_PARTS, buf, f], shift_rows[:, f, :]).then_inc(shift_loaded[f], SEM_DMA)

                load_operands(0, 0)
                load_operands(1, 1)
                for k, f in enumerate(plan.before_shifts.values()):
                    shift_to_operand(f, 0, unit_base + k)

                def turn(w, buf, ends, load):
                    if load:
                        sp.wait_ge(sums_done, layer * WINDOWS * PLANS[0].n + w * plan.n + 1)
                        load_operands(w + 2, (buf + 2) % BUFS)
                    unit = unit_base + plan.units_before
                    for end in ends:
                        unit += 2
                        for dw, kind, f in end:
                            if kind == "shift":
                                shift_to_operand(f, (buf + dw) % BUFS, w * plan.units_turn + unit)
                            unit += 1

                windows(sp, lambda w, buf: turn(w, buf, plan.turn_ends, True), WINDOWS - 1 - BUFS)
                for w in range(WINDOWS - 1 - BUFS, WINDOWS - 1):
                    turn(w, w % BUFS, plan.turn_ends, w + 2 < WINDOWS)
                turn(WINDOWS - 1, (WINDOWS - 1) % BUFS, plan.last_ends, False)

            for c in range(CHUNKS):
                sp.wait_ge(x_new, CHUNKS + c + 1)
                sp.dma_start(out_tiles[:, c * TPC:(c + 1) * TPC, :], x[:, c * TPC:(c + 1) * TPC, :]).then_inc(stored, SEM_DMA)
            sp.wait_ge(stored, CHUNKS * SEM_DMA)

        @block.gpsimd
        def _(pool):
            nc.gpsimd.memset(ident[:], 0.0).then_inc(zeroed, 1)
            nc.gpsimd.memset(mask[:], 0.0).then_inc(zeroed, 1)
            nc.gpsimd.memset(key_mask[:], 0.0).then_inc(zeroed, 1)
            nc.gpsimd.memset(ones[:], 1.0)
            nc.gpsimd.memset(power[:], -0.5)
            nc.gpsimd.memset(zeros[:], 0.0)
            pool.wait_ge(zeroed, 3)
            nc.gpsimd.affine_select(out=ident[:], in_=ident[:], compare_op=ALU.not_equal, fill=1.0, base=0,
                                    pattern=[[-1, P]], channel_multiplier=1).then_inc(zeroed, 1)
            nc.gpsimd.affine_select(out=mask[:, CHUNK - P:], in_=mask[:, CHUNK - P:], compare_op=ALU.is_ge, fill=MASKED, base=0,
                                    pattern=[[-1, P]], channel_multiplier=1)
            nc.gpsimd.affine_select(out=key_mask[:], in_=key_mask[:], compare_op=ALU.is_ge, fill=MASKED, base=0,
                                    pattern=[[1, P]], channel_multiplier=-1)
            pool.wait_ge(zeroed, 4)
            nc.gpsimd.tensor_copy(ident_bf[:], ident[:]).then_inc(consts_ready, 1)

            def inverse_deviation(k, at, count):
                pool.wait_ge(var_ready[k], count)
                nc.gpsimd.tensor_tensor(moments[:, at, 1], moments[:, at, 5], power[:], ALU.pow).then_inc(rstd_ready[k], 1)

            def third_part(g, buf):
                pool.wait_ge(part2_ready, g + 1)
                wait(pool, parts_stored[buf], (g - buf) * (STORES // 2))
                nc.gpsimd.tensor_tensor(parts[:, buf, 2], rem[:, buf], parts[:, buf, 1], ALU.subtract).then_inc(part3_ready, 1)

            nc.gpsimd.memset(v[:], 1.0).then_inc(operands_zeroed, 1)
            inverse_deviation(0, 0, 1)
            inverse_deviation(0, 1, 2)

            def first_chunk(n, buf, m):
                if m + 2 < CHUNKS:
                    inverse_deviation(0, buf, n + 3)
                third_part(n, buf)

            pipeline(pool, first_chunk)

            for layer, plan in enumerate(PLANS):
                pool.wait_ge(v_ready, (layer + 1) * CHUNKS)
                sums_base = layer * WINDOWS * PLANS[0].n
                half_base = layer * 2 * WINDOWS

                def copy_v(w, buf):
                    nc.gpsimd.tensor_copy(vwin[:, buf, :], v[:, bass.ds(w * VW, VW + VPAD)]).then_inc(vwin_ready, 1)

                def split_shift(w, f):
                    half = half_base + 2 * w + f
                    pool.wait_ge(negmax_ready, half + 1)
                    nc.gpsimd.tensor_tensor(shift[:, f, 0, :], negmax[:, f, :], zeros[:], ALU.add).then_inc(shift_begun, 1)
                    pool.wait_ge(shift_begun, half + 1)
                    nc.gpsimd.tensor_tensor(shift[:, f, 1, :], negmax[:, f, :], shift[:, f, 0, :], ALU.subtract).then_inc(shift_ready, 1)

                copy_v(0, 0)
                copy_v(1, 1)
                for f in plan.before_shifts.values():
                    split_shift(0, f)
                pool.wait_ge(xn_ready[0], (layer + 1) * CHUNKS)
                nc.gpsimd.tensor_tensor(x[:], x[:], bvo[:, layer, 1:2, :].broadcast_to([P, TILES, E]), ALU.add).then_inc(x_biased, 1)

                def turn(w, buf, ends, copy):
                    if copy:
                        pool.wait_ge(sums_done, sums_base + w * plan.n + 1)
                        copy_v(w + 2, (buf + 2) % BUFS)
                    for end in ends:
                        for dw, kind, f in end:
                            if kind == "shift":
                                split_shift(w + dw, f)

                windows(pool, lambda w, buf: turn(w, buf, plan.turn_ends, True), WINDOWS - 1 - BUFS)
                for w in range(WINDOWS - 1 - BUFS, WINDOWS - 1):
                    turn(w, w % BUFS, plan.turn_ends, w + 2 < WINDOWS)
                turn(WINDOWS - 1, (WINDOWS - 1) % BUFS, plan.last_ends, False)
                pool.wait_ge(att_ready, half_base + 2 * WINDOWS + 2)

                def middle(n, buf, m):
                    out_stage, _, _, qkv_stage = stages(layer, m)
                    g = layer * CHUNKS + n
                    if qkv_stage:
                        inverse_deviation(0, buf, g + CHUNKS + 1)
                    if out_stage:
                        wait(pool, ot_psum, g + 2)
                        windows_of = bass.ds((n + 2 - buf) * (GROUPS // 2), GROUPS) if not isinstance(n, int) else \
                            slice((n + 2) // 2 * GROUPS, ((n + 2) // 2 + 1) * GROUPS)
                        src = att[:, windows_of, TPC * buf:TPC * (buf + 1), :].rearrange("p g t e -> p t g e")
                        nc.gpsimd.tensor_copy(ot[:].rearrange("p t (g e) -> p t g e", g=GROUPS), src).then_inc(ot_ready, 1)
                        inverse_deviation(1, 2, g + 3)
                    if qkv_stage:
                        third_part(g + CHUNKS, buf)

                pipeline(pool, middle, -2)

        @block.scalar
        def _(act):
            act.wait_ge(setup_psum, 1)
            nc.scalar.copy(bqk[:].rearrange("p l t -> p (l t)"), psum[:, 0, 0:4])
            nc.scalar.copy(bvo[:].rearrange("p l t e -> p (l t e)"), psum[:, 1, :]).then_inc(setup_ready, 1)
            for k in range(3):
                act.wait_ge(setup_psum, 2 + k)
                nc.scalar.copy(wffn[:, k].rearrange("p c d -> p (c d)"), psum[:, 2 + k, 0:HIDDEN]).then_inc(setup_ready, 1)

            def copy_xt(g, buf, bank):
                act.wait_ge(xt_psum[0], g + 1)
                wait(act, qkv_psum, 3 * (g - 1))
                nc.scalar.copy(xt[:, buf, :], psum[:, bank, :]).then_inc(xt_ready[0], 1)

            def take_qk(layer, g, buf, banks):
                for t in range(2):
                    act.wait_ge(qkv_psum, 3 * g + t + 1)
                    if t == 0:
                        wait(act, rem_ready, g - 1)
                        wait(act, parts_stored[buf], (g - buf) * (STORES // 2))
                    src, bias = psum[:, banks + t, :], bqk[:, layer, t:t + 1]
                    nc.scalar.activation(qk[:, buf, t, :], src, ACT.Identity, bias=bias).then_inc(qk_ready, 1)
                    nc.scalar.activation(parts[:, buf, 0, t, :], src, ACT.Identity, bias=bias).then_inc(qk_ready, 1)

            copy_xt(0, 0, 0)

            def first_chunk(n, buf, m):
                if m + 1 < CHUNKS:
                    copy_xt(n + 1, 1 - buf, 1 - buf)
                take_qk(0, n, buf, 2 + 3 * buf)

            pipeline(act, first_chunk)

            for layer, plan in enumerate(PLANS):
                unit_base = layer * PLANS[0].units_all
                sums_base = layer * WINDOWS * PLANS[0].n
                half_base = layer * 2 * WINDOWS

                def exp_units(w, wmod, s, unit, static_unit):
                    f, j, c0 = plan.steps[s]
                    for pair in range(2):
                        bank = 2 * ((static_unit + pair) % 2)
                        slot = (wmod * 2 * plan.n + 2 * s + pair) % PROBS
                        act.wait_ge(scores_ready, unit + pair + 1)
                        if pair == 0:
                            before = w * plan.n + s + 1 - PROBS // 2
                            if not (isinstance(before, int) and before <= 0):
                                act.wait_ge(sums_done, sums_base + before)
                        nc.scalar.activation(probs[:, slot, :, c0:], psum[:, bank:bank + 2, c0:], ACT.Exp,
                                             scale=SCORE_SCALE).then_inc(probs_ready, 1)

                def copy_sums(w, f):
                    act.wait_ge(sums_done, sums_base + w * plan.n + plan.half_end[f] + 1)
                    nc.scalar.copy(sums[:, f, :], psum[:, 7, :]).then_inc(sums_ready, 1)

                def copy_unit(w, kind, f, unit, static_unit):
                    bank = 2 * (static_unit % 2)
                    act.wait_ge(scores_ready, unit + 1)
                    if kind == "shift":
                        rows = SHIFT_PARTS * HG * TPC
                        nc.scalar.copy(shift_rows[:, f, :], psum[0:rows, bank, 0:P // 2].bitcast(BF16)).then_inc(probs_ready, 1)
                    else:
                        act.wait_ge(att_ready, half_base + 2 * w + f + 1)
                        src = psum[:, bank, :].rearrange("p (t h m) -> p t h m", t=TPC, h=HG)[:, :, :, 0:VH]
                        nc.scalar.copy(att_raw[:, f], src).then_inc(probs_ready, 1)

                def turn(w, buf, steps, ends, unit, static_unit):
                    for (dw, s), end in zip(steps, ends):
                        exp_units(w + dw, (buf + dw) % BUFS, s, unit, static_unit)
                        if s == plan.half_start[1]:
                            copy_sums(w + dw, 0)
                        if dw == 1 and s == 0:
                            copy_sums(w, 1)
                        unit, static_unit = unit + 2, static_unit + 2
                        for jw, kind, f in end:
                            copy_unit(w + jw, kind, f, unit, static_unit)
                            unit, static_unit = unit + 1, static_unit + 1
                    return unit, static_unit

                unit = unit_base
                for f in plan.before_shifts.values():
                    copy_unit(0, "shift", f, unit, unit)
                    unit += 1
                for s in range(plan.turn):
                    exp_units(0, 0, s, unit, unit)
                    unit += 2
                windows(act, lambda w, buf: turn(w, buf, plan.turn_steps, plan.turn_ends, w * plan.units_turn + unit,
                                                 buf * plan.units_turn + unit), WINDOWS - 1)
                last, last_buf = WINDOWS - 1, (WINDOWS - 1) % BUFS
                unit += last * plan.units_turn
                unit, _ = turn(last, last_buf, plan.turn_steps[:plan.n - plan.turn], plan.last_ends, unit, unit)
                copy_sums(last, 1)
                copy_unit(last, "norm", 1, unit, unit)

                def silu(g, buf, c):
                    act.wait_ge(gate_up_psum, 2 * FB * g + 2 * c + 1)
                    if c == 0:
                        wait(act, down_psum, g)
                    nc.scalar.activation(hid[:, c, :], psum[:, 2 + 2 * (c % 2), :], ACT.Silu).then_inc(silu_ready, 1)

                def middle(n, buf, m):
                    out_stage, ffn_stage, _, qkv_stage = stages(layer, m)
                    g = layer * CHUNKS + n
                    if ffn_stage:
                        silu(g + 1, buf, 0)
                        silu(g + 1, buf, 1)
                    if out_stage:
                        act.wait_ge(ot_psum, g + 3)
                        wait(act, oproj_psum, g + 2)
                        nc.scalar.copy(ot_t[:], psum[:, 0, :]).then_inc(ot_t_ready, 1)
                    if ffn_stage:
                        silu(g + 1, buf, 2)
                    if qkv_stage:
                        copy_xt(g + CHUNKS, buf, 1)
                        take_qk(1, g + CHUNKS, buf, 4)
                    if out_stage:
                        act.wait_ge(xt_psum[1], g + 3)
                        wait(act, gate_up_psum, 2 * FB * (g + 2))
                        nc.scalar.copy(ffn_xt[:], psum[:, 0, :]).then_inc(xt_ready[1], 1)

                pipeline(act, middle, -2)

        @block.vector
        def _(dve):
            dve.sem_inc(att_ready, 2)
            dve.wait_ge(weights_loaded, 11 * SEM_DMA)
            for l in range(2):
                for dst, src in ((wqkv[:, l], wqkv_raw[:, l]), (bias_row[0:1, l, 0:3], bias_raw[:, l])):
                    nc.vector.tensor_copy(dst.rearrange("p t (h d) -> p t h d", d=HD),
                                          src.rearrange("p (h t d) -> p t h d", t=3, d=HD))
            nc.vector.tensor_scalar(wflt, wint, DEQUANT, None, ALU.mult).then_inc(wflt_ready, 1)

            def row_moments(k, at, n, count):
                st, mo = stats[:, at], moments[:, at]
                for t in range(TPC):
                    col = bass.ds(n * TPC + t, 1)
                    ins = nc.vector.bn_stats(st[:, t, :], x[:, col, :].rearrange("p o e -> p (o e)"))
                ins.then_inc(moment_steps[k], 1)
                s = st.rearrange("p t s -> p s t")
                dve.wait_ge(moment_steps[k], 3 * count + 1)
                nc.vector.tensor_tensor(mo[:, 2], s[:, 1], s[:, 4], ALU.add)
                nc.vector.tensor_tensor(mo[:, 3], s[:, 1], s[:, 4], ALU.subtract)
                nc.vector.tensor_tensor(mo[:, 4], s[:, 2], s[:, 5], ALU.add).then_inc(moment_steps[k], 1)
                dve.wait_ge(moment_steps[k], 3 * count + 2)
                nc.vector.tensor_scalar(mo[:, 0], mo[:, 2], 0.5, None, ALU.mult)
                nc.vector.tensor_scalar(mo[:, 4], mo[:, 4], 1.0 / E, EPS, ALU.mult, ALU.add)
                nc.vector.scalar_tensor_tensor(out=mo[:, 3], in0=mo[:, 3], scalar=0.25, in1=mo[:, 3],
                                               op0=ALU.mult, op1=ALU.mult).then_inc(moment_steps[k], 1)
                dve.wait_ge(moment_steps[k], 3 * count + 3)
                nc.vector.tensor_tensor(mo[:, 5], mo[:, 3], mo[:, 4], ALU.add).then_inc(var_ready[k], 1)

            def normalise(k, at, n, count, out, before):
                dve.wait_ge(rstd_ready[k], count + 1)
                wait(dve, xt_psum[k], before)
                for t in range(TPC):
                    col = bass.ds(n * TPC + t, 1)
                    ins = nc.vector.tensor_scalar(out[:, t, :], x[:, col, :].rearrange("p o e -> p (o e)"),
                                                  moments[:, at, 0, t:t + 1], moments[:, at, 1, t:t + 1], ALU.subtract, ALU.mult)
                ins.then_inc(xn_ready[k], 1)

            def add_to_x(n, bank, done):
                tiles = bass.ds(n * TPC, TPC)
                nc.vector.tensor_tensor(x[:, tiles, :], psum[:, bank, :].rearrange("p (t e) -> p t e", e=E), x[:, tiles, :],
                                        ALU.add).then_inc(done, 1)

            def split_chunk(layer, n, buf, v_bank):
                g = layer * CHUNKS + n
                dve.wait_ge(qk_ready, 4 * (g + 1))
                wait(dve, part3_ready, g - 1)
                nc.vector.tensor_tensor(rem[:, buf], qk[:, buf], parts[:, buf, 0], ALU.subtract).then_inc(rem_ready, 1)
                dve.wait_ge(rem_ready, g + 1)
                wait(dve, parts_stored[buf], (g - buf) * (STORES // 2))
                nc.vector.tensor_copy(parts[:, buf, 1], rem[:, buf]).then_inc(part2_ready, 1)
                dve.wait_ge(qkv_psum, 3 * (g + 1))
                bv = bvo[:, layer, 0, :].rearrange("p (g c d) -> p g c d", g=GROUPS, d=HD)
                vb = v[:, bass.ds((n - buf) * (GROUPS * VW // 2), GROUPS * VW)].rearrange("p (g k c d) -> p g k c d", g=GROUPS, k=KB, d=VH)
                for t in range(TPC):
                    src = psum[:, v_bank, t * P:(t + 1) * P].rearrange("p (g c d) -> p g c d", g=GROUPS, d=HD)
                    ins = nc.vector.tensor_tensor(vb[:, :, TPC * buf + t, :, 0:HD], src, bv, ALU.add)
                ins.then_inc(v_ready, 1)

            dve.wait_ge(x_loaded, CHUNKS * SEM_DMA)
            for n in range(2):
                row_moments(0, n, n, n)
                normalise(0, n, n, n, xn[:, n], 0)
            dve.wait_ge(setup_ready, 4)
            dve.wait_ge(operands_zeroed, 1)

            def first_chunk(n, buf, m):
                if m + 2 < CHUNKS:
                    row_moments(0, buf, n + 2, n + 2)
                split_chunk(0, n, buf, 4 + 3 * buf)
                if m + 2 < CHUNKS:
                    normalise(0, buf, n + 2, n + 2, xn[:, buf], n + 1)

            pipeline(dve, first_chunk)
            nc.vector.memset(qop[64:P], 0.0).then_inc(ones_ready, 1)
            nc.vector.memset(kop[64:P], 0.0).then_inc(ones_ready, 1)
            dve.wait_ge(ones_ready, 2)
            nc.vector.memset(kop[SHIFT_ROW:SHIFT_ROW + SHIFT_PARTS], 1.0).then_inc(ones_ready, 1)

            for layer, plan in enumerate(PLANS):
                job_base = layer * PLANS[0].jobs_all
                unit_base = layer * PLANS[0].units_all
                half_base = layer * 2 * WINDOWS

                def run_job(job, index, static_index):
                    f, c, qb, kh, width, diagonal = job
                    slot = static_index % RING
                    src, dst = psum[:, 4 + slot, 0:width], maxima[:, f, c, qb, kh:kh + 1]
                    dve.wait_ge(ring_full, index + 1)
                    if diagonal:
                        dve.sem_inc(begun, 1)
                        nc.vector.tensor_tensor_reduce(out=junk[:, slot, 0:width], in0=src, in1=mask[:, CHUNK - width:], scale=1.0,
                                                       scalar=LOWEST, op0=ALU.add, op1=ALU.max, accum_out=dst).then_inc(ring_free, 1)
                    else:
                        nc.vector.tensor_reduce(dst, src, AX_X, ALU.max).then_inc(ring_free, 1)

                def negate_max(f, index):
                    dve.wait_ge(ring_free, index)
                    src = maxima[:, f, :, :, 0:1] if plan.causal and f == 0 else maxima[:, f]
                    nc.vector.tensor_reduce(negmax[:, f, :].rearrange("p (h t) -> p h t", h=HG), src, AX_X, ALU.max,
                                            negate=True).then_inc(negmax_ready, 1)

                def invert_denominators(w, f, unit):
                    dve.wait_ge(probs_ready, unit + 1)
                    nc.vector.reciprocal(rden[:, f], att_raw[:, f, :, :, HD]).then_inc(rden_ready, 1)

                def scale_sums(w, f):
                    dve.wait_ge(rden_ready, half_base + 2 * w + f + 1)
                    dst = att[:, bass.ds(w, 1), TPC * f:TPC * (f + 1), :].rearrange("p o t (h d) -> p (o t) h d", h=HG)
                    nc.vector.tensor_tensor(dst, att_raw[:, f, :, :, 0:HD],
                                            rden[:, f].rearrange("p t (h o) -> p t h o", o=1).broadcast_to([P, TPC, HG, HD]),
                                            ALU.mult).then_inc(att_ready, 1)

                def turn(w, buf, jobs, ends, index, static_index, unit):
                    norms, scales, negates = [], [], []
                    for step, end in zip(jobs, ends):
                        due_norms, norms = norms, []
                        for job_slot in step:
                            for dw, job in job_slot:
                                run_job(job, index, static_index)
                                index, static_index = index + 1, static_index + 1
                                for f in negates:
                                    negate_max(f, index - 1)
                                for f in scales:
                                    scale_sums(w, f)
                                negates, scales = [], []
                                if plan.ends_half(job):
                                    negates.append(job[0])
                        for f in negates:
                            negate_max(f, index)
                        negates = []
                        for f, u in due_norms:
                            invert_denominators(w, f, u)
                            scales.append(f)
                        unit = unit + 2
                        for jw, kind, f in end:
                            if kind == "norm":
                                norms.append((f, unit))
                            unit = unit + 1
                    for f, u in norms:
                        invert_denominators(w, f, u)
                        scales.append(f)
                    for f in scales:
                        scale_sums(w, f)
                    return index, unit

                index = job_base
                due = None
                for dw, job in plan.before:
                    run_job(job, index, index)
                    index += 1
                    if due is not None:
                        negate_max(due, index - 1)
                    due = job[0] if plan.ends_half(job) else None
                if due is not None:
                    negate_max(due, index)
                unit = unit_base + plan.units_before
                windows(dve, lambda w, buf: turn(w, buf, plan.turn_jobs, plan.turn_ends, w * plan.jobs_turn + index,
                                                 buf * plan.jobs_turn + index, w * plan.units_turn + unit), WINDOWS - 1)
                last = WINDOWS - 1
                index += last * plan.jobs_turn
                _, unit = turn(last, last % BUFS, plan.last_jobs, plan.last_ends, index, index, last * plan.units_turn + unit)
                invert_denominators(last, 1, unit)
                scale_sums(last, 1)

                dve.wait_ge(x_biased, layer + 1)

                def middle(n, buf, m):
                    out_stage, ffn_stage, residual_stage, qkv_stage = stages(layer, m)
                    g = layer * CHUNKS + n
                    if residual_stage:
                        dve.wait_ge(down_psum, g + 1)
                        add_to_x(n, 7, x_new)
                    if qkv_stage:
                        dve.wait_ge(x_new, g + 1)
                        dve.sem_inc(begun, 1)
                        row_moments(0, buf, n, g + CHUNKS)

                    def gate(c):
                        dve.wait_ge(silu_ready, FB * (g + 1) + c + 1)
                        dve.wait_ge(gate_up_psum, 2 * FB * (g + 1) + 2 * c + 2)
                        nc.vector.tensor_tensor(hid[:, c, :], psum[:, 3 + 2 * (c % 2), :], hid[:, c, :], ALU.mult).then_inc(hid_ready, 1)

                    if ffn_stage:
                        gate(0)
                    if qkv_stage:
                        normalise(0, buf, n, g + CHUNKS, xn[:, buf], g + CHUNKS - 1)
                    if ffn_stage:
                        gate(1)
                        gate(2)
                    if out_stage:
                        dve.wait_ge(oproj_psum, g + 3)
                        add_to_x(n + 2, 6, x_mid)
                        dve.wait_ge(x_mid, g + 3)
                        dve.sem_inc(begun, 1)
                        row_moments(1, 2, n + 2, g + 2)
                        normalise(1, 2, n + 2, g + 2, ffn_xn, g + 2)
                    if qkv_stage:
                        if m == 0:
                            dve.wait_ge(vwin_ready, WINDOWS)
                        split_chunk(1, n, buf, 6)

                pipeline(dve, middle, -2)

        @block.tensor
        def _(pe):
            mm = nc.tensor.matmul
            pe.wait_ge(weights_loaded, 11 * SEM_DMA)
            pe.wait_ge(wflt_ready, 1)
            pe.wait_ge(consts_ready, 1)
            for l in range(2):
                for t in range(2):
                    mm(psum[:, 0, 2 * l + t:2 * l + t + 1], bias_row[0:1, l, t, :], ones[0:1, 0:1], start=True, stop=True)
            for l in range(2):
                mm(psum[:, 1, 2 * l * E:2 * l * E + E], ones[0:1, :], bias_row[0:1, l, 2, :], start=True, stop=True)
                ins = mm(psum[:, 1, 2 * l * E + E:2 * l * E + 2 * E], ones[0:1, :], bias_row[0:1, l, 3, :], start=True, stop=True)
            ins.then_inc(setup_psum, 1)
            for k in range(3):
                for c in range(FB):
                    ins = nc.tensor.transpose(psum[:, 2 + k, c * P:(c + 1) * P], wflt[:, k, c, :], ident[:])
                ins.then_inc(setup_psum, 1)
            pe.wait_ge(setup_ready, 4)

            def transpose_tiles(src, bank):
                for t in range(TPC):
                    ins = nc.tensor.transpose(psum[:, bank, t * P:(t + 1) * P], src[:, t, :], ident[:])
                return ins

            def transpose_xn(g, buf, bank):
                pe.wait_ge(xn_ready[0], g + 1)
                transpose_tiles(xn[:, buf], bank).then_inc(xt_psum[0], 1)

            def qkv_products(layer, g, buf, qk_banks, v_bank):
                pe.wait_ge(xt_ready[0], g + 1)
                for t in range(2):
                    mm(psum[:, qk_banks + t, :], wqkv[:, layer, t, :], xt[:, buf, :], start=True, stop=True).then_inc(qkv_psum, 1)
                for t in range(TPC):
                    ins = mm(psum[:, v_bank, t * P:(t + 1) * P], xt[:, buf, t * P:(t + 1) * P], wqkv[:, layer, 2, :],
                             start=True, stop=True)
                ins.then_inc(qkv_psum, 1)

            transpose_xn(0, 0, 0)

            def first_chunk(n, buf, m):
                if m + 1 < CHUNKS:
                    wait(pe, xt_ready[0], n)
                    transpose_xn(n + 1, 1 - buf, 1 - buf)
                wait(pe, qk_ready, 4 * (n - 1))
                wait(pe, v_ready, n - 1)
                qkv_products(0, n, buf, 2 + 3 * buf, 4 + 3 * buf)

            pipeline(pe, first_chunk)
            pe.wait_ge(ones_ready, 3)

            for layer, plan in enumerate(PLANS):
                pe.wait_ge(qk_ready, 4 * (layer + 1) * CHUNKS)
                pe.wait_ge(v_ready, (layer + 1) * CHUNKS)

                job_base = layer * PLANS[0].jobs_all
                unit_base = layer * PLANS[0].units_all
                sums_base = layer * WINDOWS * PLANS[0].n
                half_base = layer * 2 * WINDOWS

                def run_job(w, buf, job, index, static_index):
                    f, c, qb, kh, width, _ = job
                    slot = 4 + static_index % RING
                    wait(pe, ring_free, index - RING + 1)
                    if (f, c, qb, kh) == (0, 0, 0, 0):
                        earlier = layer * len(range(buf, WINDOWS, BUFS))
                        pe.wait_ge(operands_loaded[buf], (w - buf) * (LOADS // BUFS) + (earlier + 1) * LOADS)
                    mm(psum[:, slot, 0:width], qop[0:SHIFT_ROW, buf, f, c, qb * P:(qb + 1) * P], kop[0:SHIFT_ROW, buf, c, kh * CHUNK:kh * CHUNK + width],
                       start=True, stop=True).then_inc(ring_full, 1)

                def scores(w, buf, s, pair, unit, static_unit):
                    f, j, c0 = plan.steps[s]
                    bank = 2 * (static_unit % 2)
                    if s == plan.half_start[f] and pair == 0:
                        pe.wait_ge(shift_loaded[f], (layer * WINDOWS + w + 1) * SEM_DMA)
                    wait(pe, probs_ready, unit - 1)
                    diagonal = plan.causal and j * P >= f * CHUNK
                    for h in range(2):
                        c = 2 * pair + h
                        ins = mm(psum[:, bank + h, c0:], kop[:, buf, c, j * P:(j + 1) * P], qop[:, buf, f, c, c0:],
                                 start=True, stop=not diagonal)
                        if diagonal:
                            ins = mm(psum[:, bank + h, c0:c0 + P], ident_bf[:], key_mask[:], start=False, stop=True)
                    ins.then_inc(scores_ready, 1)

                def transpose_unit(w, kind, f, unit, static_unit):
                    bank = 2 * (static_unit % 2)
                    half = half_base + 2 * w + f
                    wait(pe, probs_ready, unit - 1)
                    if kind == "shift":
                        pe.wait_ge(shift_ready, half + 1)
                        nc.tensor.transpose(psum[0:SHIFT_PARTS * HG * TPC, bank, 0:P // 2].bitcast(BF16),
                                            shift[:, f].rearrange("p k n -> p (k n)"), ident_bf[:]).then_inc(scores_ready, 1)
                    else:
                        pe.wait_ge(sums_ready, half + 1)
                        transpose_tiles(sums[:, f, :].rearrange("p (t q) -> p t q", t=TPC), bank).then_inc(scores_ready, 1)

                def weighted_sums(w, buf, s, unit):
                    f, j, c0 = plan.steps[s]
                    if s == 0:
                        pe.wait_ge(vwin_ready, layer * WINDOWS + w + 1)
                    if s == plan.half_start[f]:
                        wait(pe, sums_ready, half_base + 2 * w + f)
                    pe.wait_ge(probs_ready, unit + 2)
                    for c in range(HG):
                        slot = (buf * 2 * plan.n + 2 * s + c // 2) % PROBS
                        at = (j * HG + c) * VH
                        ins = mm(psum[32 * c:32 * c + 32, 7, c0:], vwin[:, buf, at:at + 32], probs[:, slot, c % 2, c0:],
                                 start=(j == 0), stop=(s == plan.half_end[f]), tile_position=(0, 32 * c))
                    ins.then_inc(sums_done, 1)

                def turn(w, buf, steps, jobs, ends, index, static_index, unit, static_unit):
                    prev = (0, plan.turn - 1, unit - 2)
                    for (dw, s), slots, end in zip(steps, jobs, ends):
                        for part in range(4):
                            for jw, job in slots[part]:
                                run_job(w + jw, (buf + jw) % BUFS, job, index, static_index)
                                index, static_index = index + 1, static_index + 1
                            if part < 2:
                                scores(w + dw, (buf + dw) % BUFS, s, part, unit + part, static_unit + part)
                            elif part == 2:
                                weighted_sums(w + prev[0], (buf + prev[0]) % BUFS, prev[1], prev[2])
                        prev = (dw, s, unit)
                        unit, static_unit = unit + 2, static_unit + 2
                        for jw, kind, f in end:
                            transpose_unit(w + jw, kind, f, unit, static_unit)
                            unit, static_unit = unit + 1, static_unit + 1
                    return index, unit, prev

                index, unit = job_base, unit_base
                for k, (dw, job) in enumerate(plan.before):
                    run_job(0, 0, job, index, index)
                    index += 1
                    if k in plan.before_shifts:
                        transpose_unit(0, "shift", plan.before_shifts[k], unit, unit)
                        unit += 1
                for s in range(plan.turn):
                    scores(0, 0, s, 0, unit, unit)
                    scores(0, 0, s, 1, unit + 1, unit + 1)
                    if s:
                        weighted_sums(0, 0, s - 1, unit - 2)
                    unit += 2
                windows(pe, lambda w, buf: turn(w, buf, plan.turn_steps, plan.turn_jobs, plan.turn_ends,
                                                w * plan.jobs_turn + index, buf * plan.jobs_turn + index,
                                                w * plan.units_turn + unit, buf * plan.units_turn + unit), WINDOWS - 1)
                last, last_buf = WINDOWS - 1, (WINDOWS - 1) % BUFS
                index, unit = index + last * plan.jobs_turn, unit + last * plan.units_turn
                index, unit, prev = turn(last, last_buf, plan.turn_steps[:plan.n - plan.turn], plan.last_jobs, plan.last_ends,
                                         index, index, unit, unit)
                weighted_sums(last, last_buf, plan.n - 1, prev[2])
                transpose_unit(last, "norm", 1, unit, unit)
                pe.wait_ge(ring_free, job_base + plan.jobs_all)
                pe.wait_ge(probs_ready, unit_base + plan.units_all)

                def middle(n, buf, m):
                    out_stage, ffn_stage, _, qkv_stage = stages(layer, m)
                    g = layer * CHUNKS + n
                    if ffn_stage:
                        pe.wait_ge(xt_ready[1], g + 2)

                    def gate_up(c):
                        wait(pe, hid_ready, FB * (g + 1) + (0 if c < 2 else 1))
                        for k in range(2):
                            mm(psum[:, 2 + 2 * (c % 2) + k, :], wffn[:, k, c, :], ffn_xt[:], start=True, stop=True).then_inc(gate_up_psum, 1)

                    def down(tiles):
                        for t in tiles:
                            for c in range(FB):
                                ins = mm(psum[:, 7, t * P:(t + 1) * P], hid[:, c, t * P:(t + 1) * P], wffn[:, 2, c, :],
                                         start=(c == 0), stop=(c == FB - 1))
                        return ins

                    if ffn_stage:
                        gate_up(0)
                        if layer == 0:
                            wait(pe, qk_ready, 4 * (g + CHUNKS))
                        gate_up(1)
                    if out_stage:
                        pe.wait_ge(ot_ready, g + 3)
                        wait(pe, xt_ready[1], g + 2)
                        transpose_tiles(ot, 0).then_inc(ot_psum, 1)
                    if ffn_stage:
                        gate_up(2)
                    if qkv_stage:
                        wait(pe, xt_ready[0], g + CHUNKS)
                        transpose_xn(g + CHUNKS, buf, 1)
                    if out_stage:
                        pe.wait_ge(ot_t_ready, g + 3)
                        if layer == 0:
                            wait(pe, v_ready, g + CHUNKS)
                        wait(pe, x_mid, g + 2)
                        for t in range(TPC):
                            ins = mm(psum[:, 6, t * P:(t + 1) * P], ot_t[:, t * P:(t + 1) * P], wout[:, layer, :], start=True, stop=True)
                        ins.then_inc(oproj_psum, 1)
                    if qkv_stage:
                        if ffn_stage:
                            pe.wait_ge(hid_ready, FB * (g + 1) + 2)
                        if out_stage:
                            pe.wait_ge(x_mid, g + 3)
                        qkv_products(1, g + CHUNKS, buf, 4, 6)
                    if ffn_stage:
                        pe.wait_ge(hid_ready, FB * (g + 2))
                        wait(pe, x_new, g + 1)
                        down(range(TPC // 2))
                    if out_stage:
                        pe.wait_ge(xn_ready[1], g + 3)
                        transpose_tiles(ffn_xn, 0).then_inc(xt_psum[1], 1)
                    if ffn_stage:
                        down(range(TPC // 2, TPC)).then_inc(down_psum, 1)

                pipeline(pe, middle, -2)
                pe.wait_ge(x_new, (layer + 1) * CHUNKS)


_INS = ["L0_attn_a_x", "L0_attn_a_Wqkv", "L0_attn_a_bqkv", "L0_attn_a_Wout", "L0_attn_a_bout",
        "L0_attn_b_W_qkv", "L0_attn_b_b_qkv", "L0_attn_b_W_out", "L0_attn_b_b_out",
        "L0_ffn_w_gate", "L0_ffn_w_up", "L0_ffn_w_down"]


def kernel(**inputs):
    import numpy as np
    import concourse.bacc as bacc
    from concourse.bass_utils import run_bass_kernel_spmd

    nc = bacc.Bacc("TRN2", target_bir_lowering=False, num_devices=1)
    arrays, args = {}, []
    for name in _INS:
        a = np.ascontiguousarray(inputs[name])
        arrays[f"in_{name}"] = a
        args.append(nc.dram_tensor(f"in_{name}", a.shape, mybir.dt.from_np(a.dtype), kind="ExternalInput").ap())
    out = nc.dram_tensor("out_x", (B, S, E), F32, kind="ExternalOutput").ap()
    transformer_pair_kernel(nc, *args, out)
    r = run_bass_kernel_spmd(nc, [arrays], core_ids=[0])
    return r.results[0]["out_x"]
```

```python
import struct
from contextlib import ExitStack

import concourse.bass as bass
from concourse import mybir
from concourse.alu_op_type import AluOpType as ALU

ACT = mybir.ActivationFunctionType
F32 = mybir.dt.float32
BF16 = mybir.dt.bfloat16
I32 = mybir.dt.int32
AX_X = mybir.AxisListType.X

P = 128
B, S, E, H = 4, 1024, 128, 16
HD = E // H
HIDDEN = 384
FB = HIDDEN // P
EPS = 1e-5
DEQUANT = 1.0 / 127.0
SCORE_SCALE = float(HD) ** -0.5
MASKED = -1.0e30
LOWEST = -3.0e38
PAIR_OF_ONES = struct.unpack("<f", bytes.fromhex("803f803f"))[0]

TILES = B * S // P
CHUNK = 512
TPC = CHUNK // P
CHUNKS = B * S // CHUNK
KB = S // P
HG = 4
GROUPS = H // HG
WINDOWS = B * GROUPS
PARTS = 3
PD = PARTS * HD
SHIFT_ROW = 96
SHIFT_PARTS = 2
VH = HD + 1
VW = KB * HG * VH
VPAD = 32 - VH
BUFS = 3
RING = 3
PROBS = 6
SLOT_WEIGHTS = (1, 1, 1, 0)
SEM_DMA = 16


class Plan:

    def __init__(self, causal, turn, cut, idle_steps, lead, project_at):
        self.causal = causal
        self.turn = turn
        self.steps = []
        for f in range(2):
            for j in ([0, 3, 2, 1] if causal and f == 0 else range(KB)):
                c0 = max(0, j * P - f * CHUNK) if causal else 0
                if c0 < CHUNK:
                    self.steps.append((f, j, c0))
        n = self.n = len(self.steps)
        self.half_start = [0, sum(1 for s in self.steps if s[0] == 0)]
        self.half_end = [self.half_start[1] - 1, n - 1]
        stream = []
        for f in range(2):
            for qb in range(TPC):
                for c in range(HG):
                    width = (TPC * f + qb + 1) * P if causal else S
                    for kh in range(2):
                        w = min(width - kh * CHUNK, CHUNK)
                        if w > 0:
                            stream.append((f, c, qb, kh, w, causal and kh * CHUNK + w == width))
        cut = len(stream) if cut is None else cut
        jobs = [(0, x) for x in stream[cut:]] + [(1, x) for x in stream[:cut]]
        self.turn_steps = [(0, s) for s in range(turn, n)] + [(1, s) for s in range(turn)]
        slots = [0 if i >= n - idle_steps else weight * (CHUNK - self.steps[s][2])
                 for i, (_, s) in enumerate(self.turn_steps) for weight in SLOT_WEIGHTS]
        total_c, total_s = sum(x[4] for _, x in jobs), sum(slots)
        placed, k, done_c, done_s = [], 0, 0, 0
        for w in slots:
            done_s += w
            slot = []
            while k < len(jobs) and (done_c + jobs[k][1][4] / 2) * total_s <= done_s * total_c:
                slot.append(jobs[k])
                done_c += jobs[k][1][4]
                k += 1
            placed.append(slot)
        assert k == len(jobs)
        self.turn_jobs = [placed[4 * i: 4 * i + 4] for i in range(n)]
        self.turn_ends = [[] for _ in range(n)]
        for i, (dw, s) in enumerate(self.turn_steps):
            if (dw, s) == (0, self.half_end[0] + 2):
                self.turn_ends[i].append((0, "norm", 0))
            if (dw, s) == (1, 1):
                self.turn_ends[i].append((0, "norm", 1))
            for jw, x in (y for slot in self.turn_jobs[i] for y in slot):
                if self.ends_half(x):
                    self.turn_ends[i + 1].append((jw, "shift", x[0]))
        units = [("exp", s, pair) for s in range(turn) for pair in range(2)]
        events, due, start = [], {}, None
        for k, x in enumerate(stream[:cut]):
            events.append(("job", x))
            if self.ends_half(x):
                due[k + 4] = ("shift", x[0])
                start = k + 4 + lead if x[0] == 0 else start
            if k in due:
                events.append(due.pop(k))
            elif start is not None and k >= start and (k - start) % 3 == 0 and units:
                events.append(units.pop(0))
        self.before = events + units + list(due.values())
        self.project_at = project_at
        own = [i for i, (dw, _) in enumerate(self.turn_steps) if dw == 0]
        self.last_jobs = [[[x for x in slot if x[0] == 0] for slot in self.turn_jobs[i]] for i in own]
        self.last_ends = [[x for x in self.turn_ends[i] if x[0] == 0] for i in own]
        self.units_before = sum(kind != "job" for kind, *_ in self.before)
        self.units_turn = 2 * n + sum(map(len, self.turn_ends))
        self.units_all = (self.units_before + (WINDOWS - 1) * self.units_turn + 2 * len(own)
                          + sum(map(len, self.last_ends)) + 1)
        self.jobs_before, self.jobs_turn = cut, len(jobs)
        self.jobs_all = WINDOWS * len(stream)
        assert self.units_turn % 2 == 0

    def ends_half(self, job):
        f, c, qb, kh, _, _ = job
        return (c, qb, kh) == (HG - 1, TPC - 1, 0 if self.causal and f == 0 else 1)


PLANS = [Plan(causal=False, turn=3, cut=32 + 22, idle_steps=0, lead=7, project_at=(6, 8, 11)), Plan(causal=True, turn=2, cut=None, idle_steps=1, lead=12, project_at=(2, 4, 8))]


def transformer_pair_kernel(nc, x_in, wqkv_a, bqkv_a, wout_a, bout_a, wqkv_b, bqkv_b, wout_b, bout_b,
                            w_gate, w_up, w_down, out):
    x_tiles = x_in.rearrange("b (t p) e -> p (b t) e", p=P)
    out_tiles = out.rearrange("b (t p) e -> p (b t) e", p=P)
    STORES = 2 * PARTS * SEM_DMA
    LOADS = (4 * PARTS - 1) * SEM_DMA
    q_parts = nc.dram_tensor("q_parts", [WINDOWS, HG, PD, S], BF16, kind="Internal").ap()
    k_parts = nc.dram_tensor("k_parts", [WINDOWS, HG, PD, S], BF16, kind="Internal").ap()

    with ExitStack() as ctx:
        def sb(name, shape, dt):
            return ctx.enter_context(nc.sbuf_tensor(name, shape, dt))

        def sem(name):
            return ctx.enter_context(nc.semaphore(name))

        psum = ctx.enter_context(nc.psum_tensor("psum", [P, 8, CHUNK], F32))

        x = sb("x", [P, TILES, E], F32)
        first_stats = sb("first_stats", [P, TILES, 6], F32)
        first_moments = sb("first_moments", [P, 6, TILES], F32)
        stats = sb("stats", [P, 3, TPC, 6], F32)
        moments = sb("moments", [P, 3, 6, TPC], F32)
        power = sb("power", [P, TILES], F32)
        xn = sb("xn", [P, 2, TPC, E], F32)
        xt = sb("xt", [P, 2, CHUNK], F32)
        ffn_xn = sb("ffn_xn", [P, TPC, E], F32)
        ffn_xt = sb("ffn_xt", [P, CHUNK], F32)
        qk = sb("qk", [P, 2, 2, CHUNK], F32)
        rem = sb("rem", [P, 2, 2, CHUNK], F32)
        parts = sb("parts", [P, 2, PARTS, 2, CHUNK], BF16)
        v = sb("v", [P, WINDOWS * VW + VPAD], F32)
        vwin = sb("vwin", [P, BUFS, VW + VPAD], F32)
        qop = sb("qop", [P, BUFS, 2, HG, CHUNK], BF16)
        kop = sb("kop", [P, BUFS, HG, S], BF16)
        probs = sb("probs", [P, PROBS, 2, CHUNK], F32)
        junk = sb("junk", [P, RING, CHUNK], BF16)
        maxima = sb("maxima", [P, 2, HG, TPC, 2], F32)
        negmax = sb("negmax", [P, 2, HG * TPC], F32)
        zeros = sb("zeros", [P, HG * TPC], F32)
        shift = sb("shift", [P, 2, SHIFT_PARTS, HG * TPC], BF16)
        shift_rows = sb("shift_rows", [SHIFT_PARTS * HG * TPC, 2, P], BF16)
        sums = sb("sums", [P, 2, CHUNK], F32)
        att_raw = sb("att_raw", [P, 2, TPC, HG, VH], F32)
        rden = sb("rden", [P, 2, TPC, HG], F32)
        att = sb("att", [P, WINDOWS, KB, HG * HD], F32)
        ot = sb("ot", [P, TPC, E], F32)
        ot_t = sb("ot_t", [P, CHUNK], F32)
        hid = sb("hid", [P, FB, CHUNK], F32)
        wqkv = sb("wqkv", [P, 2, 3, E], F32)
        wout = sb("wout", [P, 2, E], F32)
        bias_row = sb("bias_row", [1, 2, 4, E], F32)
        bqk = sb("bqk", [P, 2, 2], F32)
        bvo = sb("bvo", [P, 2, 2, E], F32)
        early = probs[:].rearrange("p u h q -> p (u h q)")
        wsize = 3 * FB * P
        wint = early[:, 0:wsize].bitcast(I32).rearrange("p (k c d) -> p k c d", k=3, c=FB)
        wflt = early[:, wsize:2 * wsize].rearrange("p (k c d) -> p k c d", k=3, c=FB)
        wqkv_raw = early[:, 2 * wsize:2 * wsize + 6 * E].rearrange("p (l n) -> p l n", l=2)
        bias_raw = early[0:1, 2 * wsize + 6 * E:2 * wsize + 12 * E].rearrange("p (l n) -> p l n", l=2)
        wffn = sb("wffn", [P, 3, FB, P], F32)
        ident = sb("ident", [P, P], F32)
        ident_bf = sb("ident_bf", [P, P], BF16)
        ones = sb("ones", [1, P], F32)
        mask = sb("mask", [P, CHUNK], F32)
        key_mask = sb("key_mask", [P, P], BF16)

        x_loaded = [sem(f"x_loaded{k}") for k in range(3)]
        qkv_weights_loaded = sem("qkv_weights_loaded")
        other_weights_loaded = sem("other_weights_loaded")
        zeroed = sem("zeroed")
        consts_ready = sem("consts_ready")
        v_set = sem("v_set")
        operands_zeroed = sem("operands_zeroed")
        ones_ready = sem("ones_ready")
        wqkv_ready = sem("wqkv_ready")
        wflt_ready = sem("wflt_ready")
        setup_psum = sem("setup_psum")
        setup_ready = sem("setup_ready")
        moment_steps = [sem(f"moment_steps{k}") for k in range(3)]
        var_ready = [sem(f"var_ready{k}") for k in range(3)]
        rstd_ready = [sem(f"rstd_ready{k}") for k in range(3)]
        xn_ready = [sem(f"xn_ready{k}") for k in range(2)]
        xt_psum = [sem(f"xt_psum{k}") for k in range(2)]
        xt_ready = [sem(f"xt_ready{k}") for k in range(2)]
        qkv_psum = sem("qkv_psum")
        qk_ready = sem("qk_ready")
        part1_ready = sem("part1_ready")
        rem_ready = sem("rem_ready")
        part2_ready = sem("part2_ready")
        part3_ready = sem("part3_ready")
        v_ready = sem("v_ready")
        parts_stored = [sem(f"parts_stored{p}") for p in range(2)]
        operands_loaded = [sem(f"operands_loaded{p}") for p in range(BUFS)]
        vwin_ready = sem("vwin_ready")
        x_biased = sem("x_biased")
        ring_full = sem("ring_full")
        ring_free = sem("ring_free")
        begun = sem("begun")
        negmax_ready = sem("negmax_ready")
        shift_begun = sem("shift_begun")
        shift_ready = sem("shift_ready")
        shift_loaded = [sem(f"shift_loaded{f}") for f in range(2)]
        scores_ready = sem("scores_ready")
        probs_ready = sem("probs_ready")
        sums_done = sem("sums_done")
        sums_ready = sem("sums_ready")
        rden_ready = sem("rden_ready")
        att_ready = sem("att_ready")
        ot_ready = sem("ot_ready")
        ot_psum = sem("ot_psum")
        ot_t_ready = sem("ot_t_ready")
        oproj_psum = sem("oproj_psum")
        x_mid = sem("x_mid")
        gate_up_psum = sem("gate_up_psum")
        silu_ready = sem("silu_ready")
        hid_ready = sem("hid_ready")
        down_psum = sem("down_psum")
        x_new = sem("x_new")
        stored = sem("stored")

        def wait(eng, s, value):
            if isinstance(value, int) and value <= 0:
                return
            eng.wait_ge(s, value)

        def windows(eng, body, turns):
            assert turns % BUFS == 0
            with eng.Fori(0, turns // BUFS) as i:
                for p in range(BUFS):
                    body(i * BUFS + p, p, i)

        def pipeline(eng, body, first=0):
            for n in range(first, 2):
                body(n, n % 2, n)
            with eng.Fori(1, CHUNKS // 2 - 1) as i:
                for p in range(2):
                    body(i * 2 + p, p, 2)
            for n in range(CHUNKS - 2, CHUNKS):
                body(n, n % 2, n)

        def stages(layer, m):
            return m + 2 < CHUNKS, 0 <= m + 1 < CHUNKS, m >= 0, m >= 0 and layer == 0

        block = ctx.enter_context(nc.Block())

        @block.sync
        def _(sp):
            def load_x(c, loaded):
                sp.dma_start(x[:, c * TPC:(c + 1) * TPC, :], x_tiles[:, c * TPC:(c + 1) * TPC, :]).then_inc(loaded, SEM_DMA)

            load_x(0, x_loaded[0])
            for l, (w, b, bo) in enumerate(((wqkv_a, bqkv_a, bout_a), (wqkv_b, bqkv_b, bout_b))):
                sp.dma_start(wqkv_raw[:, l, :], w).then_inc(qkv_weights_loaded, SEM_DMA)
                sp.dma_start(bias_raw[0:1, l, :], b.rearrange("(o n) -> o n", o=1)).then_inc(qkv_weights_loaded, SEM_DMA)
                sp.dma_start(bias_row[0:1, l, 3, :], bo.rearrange("(o n) -> o n", o=1)).then_inc(qkv_weights_loaded, SEM_DMA)
            load_x(1, x_loaded[1])
            for c in range(2, CHUNKS):
                load_x(c, x_loaded[2])
            for k, w in enumerate((w_gate, w_up)):
                sp.dma_start(wint[:, k], w.rearrange("(c p) d -> p c d", p=P)).then_inc(other_weights_loaded, SEM_DMA)
            sp.dma_start(wint[:, 2], w_down.rearrange("d (c p) -> d c p", p=P)).then_inc(other_weights_loaded, SEM_DMA)
            for l, w in enumerate((wout_a, wout_b)):
                sp.dma_start(wout[:, l, :], w).then_inc(other_weights_loaded, SEM_DMA)

            def store_parts(layer, i, half):
                n = layer * CHUNKS + i * 2 + half
                cols, sequence = slice(half * CHUNK, (half + 1) * CHUNK), bass.ds(i, 1)
                q_dst = q_parts.rearrange("(b g) h (i d) t -> b i (g h) d t", g=GROUPS, d=HD)
                k_dst = k_parts.rearrange("(b g) h (i d) t -> b i (g h) d t", g=GROUPS, d=HD)
                for k, ready in enumerate((part1_ready, part2_ready, part3_ready)):
                    sp.wait_ge(ready, n + 1)
                    sp.dma_start(q_dst[sequence, k, :, :, cols].rearrange("o h d t -> (o h) d t"),
                                 parts[:, half, k, 0, :]).then_inc(parts_stored[half], SEM_DMA)
                    sp.dma_start(k_dst[sequence, k, :, :, cols].rearrange("o h d t -> (o h) d t"),
                                 parts[:, half, k, 1, :]).then_inc(parts_stored[half], SEM_DMA)

            def load_operands(w, buf):
                for s in range(PARTS):
                    rows = slice(s * PD, (s + 1) * PD)
                    for f in range(2):
                        q_src = q_parts[bass.ds(w, 1), :, :, f * CHUNK:(f + 1) * CHUNK].rearrange("o h r t -> r (o h) t")
                        sp.dma_start(qop[rows, buf, f], q_src).then_inc(operands_loaded[buf], SEM_DMA)
                    k_src, split = k_parts[bass.ds(w, 1)].rearrange("o h r t -> r (o h) t"), (s + 1) * PD - s * HD
                    sp.dma_start(kop[rows.start:split, buf], k_src[s * HD:]).then_inc(operands_loaded[buf], SEM_DMA)
                    if s:
                        sp.dma_start(kop[split:rows.stop, buf], k_src[:s * HD]).then_inc(operands_loaded[buf], SEM_DMA)

            for layer, plan in enumerate(PLANS):
                with sp.Fori(0, B // 2) as i:
                    for half in range(2):
                        store_parts(layer, i, half)
                for p in range(2):
                    sp.wait_ge(parts_stored[p], (layer * B + B // 2) * STORES)
                if layer == 0:
                    sp.wait_ge(ones_ready, 1)
                load_operands(0, 0)
                with sp.Fori(B // 2, B) as i:
                    for half in range(2):
                        store_parts(layer, i, half)
                for p in range(2):
                    sp.wait_ge(parts_stored[p], (layer + 1) * B * STORES)
                load_operands(1, 1)
                unit = unit_base = layer * PLANS[0].units_all

                def shift_to_operand(f, buf, unit):
                    sp.wait_ge(probs_ready, unit + 1)
                    sp.dma_start(qop[SHIFT_ROW:SHIFT_ROW + SHIFT_PARTS, buf, f], shift_rows[:, f, :]).then_inc(shift_loaded[f], SEM_DMA)

                for kind, *what in plan.before:
                    if kind == "shift":
                        shift_to_operand(what[0], 0, unit)
                    if kind != "job":
                        unit += 1

                def turn(w, buf, ends, load):
                    if load:
                        sp.wait_ge(sums_done, layer * WINDOWS * PLANS[0].n + w * plan.n + 1)
                        load_operands(w + 2, (buf + 2) % BUFS)
                    unit = unit_base + plan.units_before
                    for end in ends:
                        unit += 2
                        for dw, kind, f in end:
                            if kind == "shift":
                                shift_to_operand(f, (buf + dw) % BUFS, w * plan.units_turn + unit)
                            unit += 1

                windows(sp, lambda w, buf, lap: turn(w, buf, plan.turn_ends, True), WINDOWS - 1 - BUFS)
                for w in range(WINDOWS - 1 - BUFS, WINDOWS - 1):
                    turn(w, w % BUFS, plan.turn_ends, w + 2 < WINDOWS)
                turn(WINDOWS - 1, (WINDOWS - 1) % BUFS, plan.last_ends, False)

            for c in range(CHUNKS):
                sp.wait_ge(x_new, CHUNKS + c + 1)
                sp.dma_start(out_tiles[:, c * TPC:(c + 1) * TPC, :], x[:, c * TPC:(c + 1) * TPC, :]).then_inc(stored, SEM_DMA)
            sp.wait_ge(stored, CHUNKS * SEM_DMA)

        @block.gpsimd
        def _(pool):
            nc.gpsimd.memset(zeros[:], 0.0).then_inc(zeroed, 1)
            nc.gpsimd.memset(ident[:], 0.0).then_inc(zeroed, 1)
            nc.gpsimd.memset(mask[:], 0.0).then_inc(zeroed, 1)
            nc.gpsimd.memset(key_mask[:], 0.0).then_inc(zeroed, 1)
            nc.gpsimd.memset(ones[:], 1.0)
            nc.gpsimd.memset(power[:], -0.5)
            pool.wait_ge(zeroed, 4)
            nc.gpsimd.affine_select(out=ident[:], in_=ident[:], compare_op=ALU.not_equal, fill=1.0, base=0,
                                    pattern=[[-1, P]], channel_multiplier=1).then_inc(zeroed, 1)
            nc.gpsimd.affine_select(out=mask[:, CHUNK - P:], in_=mask[:, CHUNK - P:], compare_op=ALU.is_ge, fill=MASKED, base=0,
                                    pattern=[[-1, P]], channel_multiplier=1)
            nc.gpsimd.affine_select(out=key_mask[:], in_=key_mask[:], compare_op=ALU.is_ge, fill=MASKED, base=0,
                                    pattern=[[1, P]], channel_multiplier=-1)
            pool.wait_ge(zeroed, 5)
            nc.gpsimd.tensor_copy(ident_bf[:], ident[:]).then_inc(consts_ready, 1)

            def inverse_deviation(k, mo, count):
                pool.wait_ge(var_ready[k], count)
                nc.gpsimd.tensor_tensor(mo[:, 1], mo[:, 5], power[:, 0:mo.shape[-1]], ALU.pow).then_inc(rstd_ready[k], 1)

            def third_part(g, buf):
                pool.wait_ge(part2_ready, g + 1)
                wait(pool, parts_stored[buf], (g - buf) * (STORES // 2))
                nc.gpsimd.tensor_tensor(parts[:, buf, 2], rem[:, buf], parts[:, buf, 1], ALU.subtract).then_inc(part3_ready, 1)

            inverse_deviation(2, first_moments[:, :, 0:TPC], 1)
            nc.gpsimd.memset(v[:], 1.0).then_inc(v_set, 1)
            inverse_deviation(2, first_moments[:, :, TPC:2 * TPC], 2)
            pool.wait_ge(operands_zeroed, 2)
            pool.wait_ge(rstd_ready[2], 2)
            nc.gpsimd.memset(kop[SHIFT_ROW:SHIFT_ROW + SHIFT_PARTS].rearrange("p u h t -> p (u h t)").bitcast(F32),
                             PAIR_OF_ONES).then_inc(ones_ready, 1)
            pool.wait_ge(ones_ready, 1)
            inverse_deviation(2, first_moments[:, :, 2 * TPC:], 3)

            pipeline(pool, lambda n, buf, m: third_part(n, buf))

            for layer, plan in enumerate(PLANS):
                pool.wait_ge(v_ready, (layer + 1) * CHUNKS)
                sums_base = layer * WINDOWS * PLANS[0].n
                half_base = layer * 2 * WINDOWS

                def copy_v(w, buf):
                    nc.gpsimd.tensor_copy(vwin[:, buf, :], v[:, bass.ds(w * VW, VW + VPAD)]).then_inc(vwin_ready, 1)

                def split_shift(w, f):
                    half = half_base + 2 * w + f
                    pool.wait_ge(negmax_ready, half + 1)
                    nc.gpsimd.tensor_tensor(shift[:, f, 0, :], negmax[:, f, :], zeros[:], ALU.add).then_inc(shift_begun, 1)
                    pool.wait_ge(shift_begun, half + 1)
                    nc.gpsimd.tensor_tensor(shift[:, f, 1, :], negmax[:, f, :], shift[:, f, 0, :], ALU.subtract).then_inc(shift_ready, 1)

                copy_v(0, 0)
                copy_v(1, 1)
                for kind, *what in plan.before:
                    if kind == "shift":
                        split_shift(0, what[0])
                pool.wait_ge(xn_ready[0], (layer + 1) * CHUNKS)
                nc.gpsimd.tensor_tensor(x[:], x[:], bvo[:, layer, 1:2, :].broadcast_to([P, TILES, E]), ALU.add).then_inc(x_biased, 1)

                def turn(w, buf, ends, copy):
                    if copy:
                        pool.wait_ge(sums_done, sums_base + w * plan.n + 1)
                        copy_v(w + 2, (buf + 2) % BUFS)
                    for end in ends:
                        for dw, kind, f in end:
                            if kind == "shift":
                                split_shift(w + dw, f)

                windows(pool, lambda w, buf, lap: turn(w, buf, plan.turn_ends, True), WINDOWS - 1 - BUFS)
                for w in range(WINDOWS - 1 - BUFS, WINDOWS - 1):
                    turn(w, w % BUFS, plan.turn_ends, w + 2 < WINDOWS)
                turn(WINDOWS - 1, (WINDOWS - 1) % BUFS, plan.last_ends, False)
                inverse_deviation(1, moments[:, 2], layer * CHUNKS + 1)

                def middle(n, buf, m):
                    out_stage, _, _, qkv_stage = stages(layer, m)
                    g = layer * CHUNKS + n
                    if qkv_stage:
                        inverse_deviation(0, moments[:, buf], g + 1)
                    if out_stage:
                        inverse_deviation(1, moments[:, 2], g + 3)
                    if qkv_stage:
                        third_part(g + CHUNKS, buf)

                pipeline(pool, middle, -1)

        @block.scalar
        def _(act):
            act.wait_ge(zeroed, 1)
            for tile in (qop[64:P].rearrange("p u f h t -> p (u f h t)"), kop[64:P].rearrange("p u h t -> p (u h t)")):
                nc.scalar.copy(tile.bitcast(F32), zeros[64:P, 0:1].broadcast_to([P - 64, BUFS * HG * S // 2])).then_inc(operands_zeroed, 1)
            act.wait_ge(setup_psum, 1)
            nc.scalar.copy(bqk[:].rearrange("p l t -> p (l t)"), psum[:, 6, 0:4])
            nc.scalar.copy(bvo[:].rearrange("p l t e -> p (l t e)"), psum[:, 7, :]).then_inc(setup_ready, 1)

            def copy_xt(g, buf, bank):
                act.wait_ge(xt_psum[0], g + 1)
                wait(act, qkv_psum, 3 * (g - 1))
                nc.scalar.copy(xt[:, buf, :], psum[:, bank, :]).then_inc(xt_ready[0], 1)

            def take_qk(layer, g, buf, banks):
                for t in range(2):
                    act.wait_ge(qkv_psum, 3 * g + t + 1)
                    if t == 0:
                        wait(act, rem_ready, g - 1)
                    nc.scalar.activation(qk[:, buf, t, :], psum[:, banks + t, :], ACT.Identity,
                                         bias=bqk[:, layer, t:t + 1]).then_inc(qk_ready, 1)
                act.wait_ge(qk_ready, 2 * (g + 1))
                wait(act, parts_stored[buf], (g - buf) * (STORES // 2))
                nc.scalar.copy(parts[:, buf, 0], qk[:, buf]).then_inc(part1_ready, 1)

            copy_xt(0, 0, 0)

            def first_chunk(n, buf, m):
                if m + 1 < CHUNKS:
                    copy_xt(n + 1, 1 - buf, 1 - buf)
                take_qk(0, n, buf, 2 + 3 * buf)

            pipeline(act, first_chunk)

            for layer, plan in enumerate(PLANS):
                unit_base = layer * PLANS[0].units_all
                sums_base = layer * WINDOWS * PLANS[0].n
                half_base = layer * 2 * WINDOWS

                def exp_unit(w, wmod, s, pair, unit, static_unit):
                    f, j, c0 = plan.steps[s]
                    bank = 2 * (static_unit % 2)
                    slot = (wmod * 2 * plan.n + 2 * s + pair) % PROBS
                    act.wait_ge(scores_ready, unit + 1)
                    if pair == 0:
                        before = w * plan.n + s + 1 - PROBS // 2
                        if not (isinstance(before, int) and before <= 0):
                            act.wait_ge(sums_done, sums_base + before)
                    nc.scalar.activation(probs[:, slot, :, c0:], psum[:, bank:bank + 2, c0:], ACT.Exp,
                                         scale=SCORE_SCALE).then_inc(probs_ready, 1)

                def copy_sums(w, f):
                    act.wait_ge(sums_done, sums_base + w * plan.n + plan.half_end[f] + 1)
                    nc.scalar.copy(sums[:, f, :], psum[:, 7, :]).then_inc(sums_ready, 1)

                def copy_unit(w, kind, f, unit, static_unit):
                    bank = 2 * (static_unit % 2)
                    act.wait_ge(scores_ready, unit + 1)
                    if kind == "shift":
                        rows = SHIFT_PARTS * HG * TPC
                        nc.scalar.copy(shift_rows[:, f, :], psum[0:rows, bank, 0:P // 2].bitcast(BF16)).then_inc(probs_ready, 1)
                    else:
                        act.wait_ge(att_ready, half_base + 2 * w + f + 1)
                        src = psum[:, bank, :].rearrange("p (t h m) -> p t h m", t=TPC, h=HG)[:, :, :, 0:VH]
                        nc.scalar.copy(att_raw[:, f], src).then_inc(probs_ready, 1)

                def gather_heads(n, buf):
                    g = layer * CHUNKS + n
                    wait(act, ot_psum, g)
                    windows_of = bass.ds((n - buf) * (GROUPS // 2), GROUPS) if not isinstance(n, int) else \
                        slice(n // 2 * GROUPS, (n // 2 + 1) * GROUPS)
                    src = att[:, windows_of, TPC * buf:TPC * (buf + 1), :].rearrange("p g t e -> p t g e")
                    nc.scalar.copy(ot[:].rearrange("p t (g e) -> p t g e", g=GROUPS), src).then_inc(ot_ready, 1)

                def copy_ot(n, bank):
                    g = layer * CHUNKS + n
                    act.wait_ge(ot_psum, g + 1)
                    wait(act, oproj_psum, g)
                    nc.scalar.copy(ot_t[:], psum[:, bank, :]).then_inc(ot_t_ready, 1)

                def copy_ffn_xt(n, bank):
                    g = layer * CHUNKS + n
                    act.wait_ge(xt_psum[1], g + 1)
                    wait(act, gate_up_psum, 2 * FB * g)
                    nc.scalar.copy(ffn_xt[:], psum[:, bank, :]).then_inc(xt_ready[1], 1)

                def early_chunk(i):
                    if i + 1 == plan.project_at[0]:
                        act.wait_ge(att_ready, half_base + 2 * GROUPS + 2)
                        gather_heads(0, 0)
                    if i == plan.project_at[0]:
                        copy_ot(0, 4)
                    if i == plan.project_at[2]:
                        copy_ffn_xt(0, 4)
                        gather_heads(1, 1)

                def turn(w, buf, steps, ends, unit, static_unit, between=None):
                    for i, ((dw, s), end) in enumerate(zip(steps, ends)):
                        for pair in range(2):
                            exp_unit(w + dw, (buf + dw) % BUFS, s, pair, unit + pair, static_unit + pair)
                        if s == plan.half_start[1]:
                            copy_sums(w + dw, 0)
                        if dw == 1 and s == 0:
                            copy_sums(w, 1)
                        unit, static_unit = unit + 2, static_unit + 2
                        for jw, kind, f in end:
                            copy_unit(w + jw, kind, f, unit, static_unit)
                            unit, static_unit = unit + 1, static_unit + 1
                        if between:
                            between(i)
                    return unit, static_unit

                if layer == 0:
                    for k in range(3):
                        act.wait_ge(setup_psum, 2 + k)
                        nc.scalar.copy(wffn[:, k].rearrange("p c d -> p (c d)"), psum[:, k, 0:HIDDEN]).then_inc(setup_ready, 1)
                unit = unit_base
                for kind, *what in plan.before:
                    if kind == "shift":
                        copy_unit(0, "shift", what[0], unit, unit)
                    elif kind == "exp":
                        exp_unit(0, 0, what[0], what[1], unit, unit)
                    if kind != "job":
                        unit += 1
                windows(act, lambda w, buf, lap: turn(w, buf, plan.turn_steps, plan.turn_ends, w * plan.units_turn + unit,
                                                 buf * plan.units_turn + unit), WINDOWS - 1)
                last, last_buf = WINDOWS - 1, (WINDOWS - 1) % BUFS
                unit += last * plan.units_turn
                unit, _ = turn(last, last_buf, plan.turn_steps[:plan.n - plan.turn], plan.last_ends, unit, unit, early_chunk)
                copy_sums(last, 1)
                copy_unit(last, "norm", 1, unit, unit)

                def silu(g, buf, c):
                    act.wait_ge(gate_up_psum, 2 * FB * g + 2 * c + 1)
                    if c == 0:
                        wait(act, down_psum, g)
                    nc.scalar.activation(hid[:, c, :], psum[:, 2 + 2 * (c % 2), :], ACT.Silu).then_inc(silu_ready, 1)

                def middle(n, buf, m):
                    out_stage, ffn_stage, _, qkv_stage = stages(layer, m)
                    g = layer * CHUNKS + n
                    if out_stage:
                        if m == 0:
                            act.wait_ge(att_ready, half_base + 2 * WINDOWS + 2)
                        if m >= 0:
                            gather_heads(n + 2, buf)
                        copy_ot(n + 2, 0)
                    if ffn_stage:
                        silu(g + 1, buf, 0)
                        silu(g + 1, buf, 1)
                        silu(g + 1, buf, 2)
                    if qkv_stage:
                        copy_xt(g + CHUNKS, buf, 1)
                        take_qk(1, g + CHUNKS, buf, 4)
                    if out_stage:
                        copy_ffn_xt(n + 2, 0)

                pipeline(act, middle, -1)

        @block.vector
        def _(dve):
            dve.sem_inc(att_ready, 2)
            def row_moments(k, st, mo, first_tile, tiles, count):
                for t in range(tiles):
                    ins = nc.vector.bn_stats(st[:, t, :], x[:, bass.ds(first_tile + t, 1), :].rearrange("p o e -> p (o e)"))
                ins.then_inc(moment_steps[k], 1)
                s = st.rearrange("p t s -> p s t")
                dve.wait_ge(moment_steps[k], 3 * count + 1)
                nc.vector.tensor_tensor(mo[:, 2], s[:, 1], s[:, 4], ALU.add)
                nc.vector.tensor_tensor(mo[:, 3], s[:, 1], s[:, 4], ALU.subtract)
                nc.vector.tensor_tensor(mo[:, 4], s[:, 2], s[:, 5], ALU.add).then_inc(moment_steps[k], 1)
                dve.wait_ge(moment_steps[k], 3 * count + 2)
                nc.vector.tensor_scalar(mo[:, 0], mo[:, 2], 0.5, None, ALU.mult)
                nc.vector.tensor_scalar(mo[:, 4], mo[:, 4], 1.0 / E, EPS, ALU.mult, ALU.add)
                nc.vector.scalar_tensor_tensor(out=mo[:, 3], in0=mo[:, 3], scalar=0.25, in1=mo[:, 3],
                                               op0=ALU.mult, op1=ALU.mult).then_inc(moment_steps[k], 1)
                dve.wait_ge(moment_steps[k], 3 * count + 3)
                nc.vector.tensor_tensor(mo[:, 5], mo[:, 3], mo[:, 4], ALU.add).then_inc(var_ready[k], 1)

            def normalise(k, n, mo, column, out, before):
                wait(dve, xt_psum[k], before)
                for t in range(TPC):
                    ins = nc.vector.tensor_scalar(out[:, t, :], x[:, bass.ds(n * TPC + t, 1), :].rearrange("p o e -> p (o e)"),
                                                  mo[:, 0, bass.ds(column + t, 1)], mo[:, 1, bass.ds(column + t, 1)],
                                                  ALU.subtract, ALU.mult)
                ins.then_inc(xn_ready[k], 1)

            def add_to_x(n, bank, done):
                tiles = bass.ds(n * TPC, TPC)
                nc.vector.tensor_tensor(x[:, tiles, :], psum[:, bank, :].rearrange("p (t e) -> p t e", e=E), x[:, tiles, :],
                                        ALU.add).then_inc(done, 1)

            def split_chunk(layer, n, buf, v_bank):
                g = layer * CHUNKS + n
                dve.wait_ge(qkv_psum, 3 * (g + 1))
                bv = bvo[:, layer, 0, :].rearrange("p (g c d) -> p g c d", g=GROUPS, d=HD)
                vb = v[:, bass.ds((n - buf) * (GROUPS * VW // 2), GROUPS * VW)].rearrange("p (g k c d) -> p g k c d", g=GROUPS, k=KB, d=VH)
                for t in range(TPC):
                    src = psum[:, v_bank, t * P:(t + 1) * P].rearrange("p (g c d) -> p g c d", g=GROUPS, d=HD)
                    ins = nc.vector.tensor_tensor(vb[:, :, TPC * buf + t, :, 0:HD], src, bv, ALU.add)
                ins.then_inc(v_ready, 1)
                dve.wait_ge(part1_ready, g + 1)
                wait(dve, part3_ready, g - 1)
                nc.vector.tensor_tensor(rem[:, buf], qk[:, buf], parts[:, buf, 0], ALU.subtract).then_inc(rem_ready, 1)
                dve.wait_ge(rem_ready, g + 1)
                wait(dve, parts_stored[buf], (g - buf) * (STORES // 2))
                nc.vector.tensor_copy(parts[:, buf, 1], rem[:, buf]).then_inc(part2_ready, 1)

            def order_columns(l):
                for dst, src in ((wqkv[:, l], wqkv_raw[:, l]), (bias_row[0:1, l, 0:3], bias_raw[:, l])):
                    ins = nc.vector.tensor_copy(dst.rearrange("p t (h d) -> p t h d", d=HD),
                                                src.rearrange("p (h t d) -> p t h d", t=3, d=HD))
                ins.then_inc(wqkv_ready, 1)

            def first_row_moments(n, chunks, count):
                tiles = slice(n * TPC, (n + chunks) * TPC)
                row_moments(2, first_stats[:, tiles], first_moments[:, :, tiles], n * TPC, chunks * TPC, count)

            dve.wait_ge(x_loaded[0], SEM_DMA)
            first_row_moments(0, 1, 0)
            dve.wait_ge(qkv_weights_loaded, 6 * SEM_DMA)
            order_columns(0)
            dve.wait_ge(rstd_ready[2], 1)
            normalise(0, 0, first_moments, 0, xn[:, 0], 0)
            order_columns(1)
            dve.wait_ge(x_loaded[1], SEM_DMA)
            first_row_moments(1, 1, 1)
            dve.wait_ge(rstd_ready[2], 2)
            normalise(0, 1, first_moments, TPC, xn[:, 1], 0)
            dve.wait_ge(x_loaded[2], (CHUNKS - 2) * SEM_DMA)
            first_row_moments(2, CHUNKS - 2, 2)
            dve.wait_ge(rstd_ready[2], 3)
            dve.wait_ge(setup_ready, 1)
            dve.wait_ge(v_set, 1)

            def first_chunk(n, buf, m):
                if m + 2 < CHUNKS:
                    normalise(0, n + 2, first_moments, (n + 2) * TPC, xn[:, buf], n + 1)
                split_chunk(0, n, buf, 4 + 3 * buf)

            pipeline(dve, first_chunk)
            dve.wait_ge(other_weights_loaded, 5 * SEM_DMA)
            nc.vector.tensor_scalar(wflt, wint, DEQUANT, None, ALU.mult).then_inc(wflt_ready, 1)

            for layer, plan in enumerate(PLANS):
                job_base = layer * PLANS[0].jobs_all
                unit_base = layer * PLANS[0].units_all
                half_base = layer * 2 * WINDOWS

                def run_job(job, index, static_index):
                    f, c, qb, kh, width, diagonal = job
                    slot = static_index % RING
                    src, dst = psum[:, 4 + slot, 0:width], maxima[:, f, c, qb, kh:kh + 1]
                    dve.wait_ge(ring_full, index + 1)
                    if diagonal:
                        dve.sem_inc(begun, 1)
                        nc.vector.tensor_tensor_reduce(out=junk[:, slot, 0:width], in0=src, in1=mask[:, CHUNK - width:], scale=1.0,
                                                       scalar=LOWEST, op0=ALU.add, op1=ALU.max, accum_out=dst).then_inc(ring_free, 1)
                    else:
                        nc.vector.tensor_reduce(dst, src, AX_X, ALU.max).then_inc(ring_free, 1)

                def negate_max(f, index):
                    dve.wait_ge(ring_free, index)
                    src = maxima[:, f, :, :, 0:1] if plan.causal and f == 0 else maxima[:, f]
                    nc.vector.tensor_reduce(negmax[:, f, :].rearrange("p (h t) -> p h t", h=HG), src, AX_X, ALU.max,
                                            negate=True).then_inc(negmax_ready, 1)

                def invert_denominators(w, f, unit):
                    dve.wait_ge(probs_ready, unit + 1)
                    nc.vector.reciprocal(rden[:, f], att_raw[:, f, :, :, HD]).then_inc(rden_ready, 1)

                def scale_sums(w, f):
                    dve.wait_ge(rden_ready, half_base + 2 * w + f + 1)
                    dst = att[:, bass.ds(w, 1), TPC * f:TPC * (f + 1), :].rearrange("p o t (h d) -> p (o t) h d", h=HG)
                    nc.vector.tensor_tensor(dst, att_raw[:, f, :, :, 0:HD],
                                            rden[:, f].rearrange("p t (h o) -> p t h o", o=1).broadcast_to([P, TPC, HG, HD]),
                                            ALU.mult).then_inc(att_ready, 1)

                def add_projection(n):
                    g = layer * CHUNKS + n
                    dve.wait_ge(oproj_psum, g + 1)
                    add_to_x(n, 6, x_mid)
                    dve.wait_ge(x_mid, g + 1)
                    dve.sem_inc(begun, 1)
                    row_moments(1, stats[:, 2], moments[:, 2], n * TPC, TPC, g)

                def normalise_rows(n):
                    g = layer * CHUNKS + n
                    dve.wait_ge(rstd_ready[1], g + 1)
                    normalise(1, n, moments[:, 2], 0, ffn_xn, g)

                def early_chunk(i):
                    if i == plan.project_at[1]:
                        dve.wait_ge(x_biased, layer + 1)
                        add_projection(0)
                        normalise_rows(0)

                def turn(w, buf, jobs, ends, index, static_index, unit, between=None):
                    norms, scales, negates = [], [], []
                    for i, (step, end) in enumerate(zip(jobs, ends)):
                        due_norms, norms = norms, []
                        for job_slot in step:
                            for dw, job in job_slot:
                                run_job(job, index, static_index)
                                index, static_index = index + 1, static_index + 1
                                for f in negates:
                                    negate_max(f, index - 1)
                                for f in scales:
                                    scale_sums(w, f)
                                negates, scales = [], []
                                if plan.ends_half(job):
                                    negates.append(job[0])
                        for f in negates:
                            negate_max(f, index)
                        negates = []
                        for f, u in due_norms:
                            invert_denominators(w, f, u)
                            scales.append(f)
                        unit = unit + 2
                        for jw, kind, f in end:
                            if kind == "norm":
                                norms.append((f, unit))
                            unit = unit + 1
                        if between:
                            between(i)
                    for f, u in norms:
                        invert_denominators(w, f, u)
                        scales.append(f)
                    for f in scales:
                        scale_sums(w, f)
                    return index, unit

                index = job_base
                due = None
                for kind, job, *_ in plan.before:
                    if kind != "job":
                        continue
                    run_job(job, index, index)
                    index += 1
                    if due is not None:
                        negate_max(due, index - 1)
                    due = job[0] if plan.ends_half(job) else None
                if due is not None:
                    negate_max(due, index)
                unit = unit_base + plan.units_before
                windows(dve, lambda w, buf, lap: turn(w, buf, plan.turn_jobs, plan.turn_ends, w * plan.jobs_turn + index,
                                                 buf * plan.jobs_turn + index, w * plan.units_turn + unit), WINDOWS - 1)
                last = WINDOWS - 1
                index += last * plan.jobs_turn
                _, unit = turn(last, last % BUFS, plan.last_jobs, plan.last_ends, index, index, last * plan.units_turn + unit, early_chunk)
                invert_denominators(last, 1, unit)
                scale_sums(last, 1)

                def middle(n, buf, m):
                    out_stage, ffn_stage, residual_stage, qkv_stage = stages(layer, m)
                    g = layer * CHUNKS + n
                    if residual_stage:
                        dve.wait_ge(down_psum, g + 1)
                        add_to_x(n, 7, x_new)
                    if qkv_stage:
                        dve.wait_ge(x_new, g + 1)
                        dve.sem_inc(begun, 1)
                        row_moments(0, stats[:, buf], moments[:, buf], n * TPC, TPC, g)

                    def gate(c):
                        dve.wait_ge(silu_ready, FB * (g + 1) + c + 1)
                        dve.wait_ge(gate_up_psum, 2 * FB * (g + 1) + 2 * c + 2)
                        nc.vector.tensor_tensor(hid[:, c, :], psum[:, 3 + 2 * (c % 2), :], hid[:, c, :], ALU.mult).then_inc(hid_ready, 1)

                    if ffn_stage:
                        gate(0)
                    if qkv_stage:
                        dve.wait_ge(rstd_ready[0], g + 1)
                        normalise(0, n, moments[:, buf], 0, xn[:, buf], g + CHUNKS - 1)
                    if out_stage:
                        add_projection(n + 2)
                    if ffn_stage:
                        gate(1)
                        gate(2)
                    if out_stage:
                        normalise_rows(n + 2)
                    if qkv_stage:
                        if m == 0:
                            dve.wait_ge(vwin_ready, WINDOWS)
                        split_chunk(1, n, buf, 1)

                pipeline(dve, middle, -1)

        @block.tensor
        def _(pe):
            mm = nc.tensor.matmul
            pe.wait_ge(consts_ready, 1)
            pe.wait_ge(wqkv_ready, 2)
            for l in range(2):
                for t in range(2):
                    mm(psum[:, 6, 2 * l + t:2 * l + t + 1], bias_row[0:1, l, t, :], ones[0:1, 0:1], start=True, stop=True)
            for l in range(2):
                mm(psum[:, 7, 2 * l * E:2 * l * E + E], ones[0:1, :], bias_row[0:1, l, 2, :], start=True, stop=True)
                ins = mm(psum[:, 7, 2 * l * E + E:2 * l * E + 2 * E], ones[0:1, :], bias_row[0:1, l, 3, :], start=True, stop=True)
            ins.then_inc(setup_psum, 1)

            def transpose_tiles(src, bank):
                for t in range(TPC):
                    ins = nc.tensor.transpose(psum[:, bank, t * P:(t + 1) * P], src[:, t, :], ident[:])
                return ins

            def transpose_xn(g, buf, bank):
                pe.wait_ge(xn_ready[0], g + 1)
                transpose_tiles(xn[:, buf], bank).then_inc(xt_psum[0], 1)

            def qkv_products(layer, g, buf, qk_banks, v_bank):
                pe.wait_ge(xt_ready[0], g + 1)
                for t in range(2):
                    mm(psum[:, qk_banks + t, :], wqkv[:, layer, t, :], xt[:, buf, :], start=True, stop=True).then_inc(qkv_psum, 1)
                for t in range(TPC):
                    ins = mm(psum[:, v_bank, t * P:(t + 1) * P], xt[:, buf, t * P:(t + 1) * P], wqkv[:, layer, 2, :],
                             start=True, stop=True)
                ins.then_inc(qkv_psum, 1)

            transpose_xn(0, 0, 0)

            def first_chunk(n, buf, m):
                if m + 1 < CHUNKS:
                    wait(pe, xt_ready[0], n)
                    transpose_xn(n + 1, 1 - buf, 1 - buf)
                wait(pe, qk_ready, 2 * (n - 1))
                wait(pe, v_ready, n - 1)
                qkv_products(0, n, buf, 2 + 3 * buf, 4 + 3 * buf)

            pe.wait_ge(setup_ready, 1)
            pipeline(pe, first_chunk)

            def transpose_weights(k):
                for c in range(FB):
                    ins = nc.tensor.transpose(psum[:, k, c * P:(c + 1) * P], wflt[:, k, c, :], ident[:])
                ins.then_inc(setup_psum, 1)

            for layer, plan in enumerate(PLANS):
                pe.wait_ge(qk_ready, 2 * (layer + 1) * CHUNKS)
                pe.wait_ge(v_ready, (layer + 1) * CHUNKS)

                job_base = layer * PLANS[0].jobs_all
                unit_base = layer * PLANS[0].units_all
                sums_base = layer * WINDOWS * PLANS[0].n
                half_base = layer * 2 * WINDOWS

                def run_job(lap, buf, job, index, static_index):
                    f, c, qb, kh, width, _ = job
                    slot = 4 + static_index % RING
                    wait(pe, ring_free, index - RING + 1)
                    if (f, c, qb, kh) == (0, 0, 0, 0):
                        earlier = layer * len(range(buf, WINDOWS, BUFS))
                        pe.wait_ge(operands_loaded[buf], (lap + earlier + 1) * LOADS)
                    mm(psum[:, slot, 0:width], qop[0:SHIFT_ROW, buf, f, c, qb * P:(qb + 1) * P], kop[0:SHIFT_ROW, buf, c, kh * CHUNK:kh * CHUNK + width],
                       start=True, stop=True).then_inc(ring_full, 1)

                def scores(w, buf, s, pair, unit, static_unit):
                    f, j, c0 = plan.steps[s]
                    bank = 2 * (static_unit % 2)
                    if s == plan.half_start[f] and pair == 0:
                        pe.wait_ge(shift_loaded[f], (layer * WINDOWS + w + 1) * SEM_DMA)
                    wait(pe, probs_ready, unit - 1)
                    diagonal = plan.causal and j * P >= f * CHUNK
                    for h in range(2):
                        c = 2 * pair + h
                        ins = mm(psum[:, bank + h, c0:], kop[:, buf, c, j * P:(j + 1) * P], qop[:, buf, f, c, c0:],
                                 start=True, stop=not diagonal)
                        if diagonal:
                            ins = mm(psum[:, bank + h, c0:c0 + P], ident_bf[:], key_mask[:], start=False, stop=True)
                    ins.then_inc(scores_ready, 1)

                def transpose_unit(w, kind, f, unit, static_unit):
                    bank = 2 * (static_unit % 2)
                    half = half_base + 2 * w + f
                    wait(pe, probs_ready, unit - 1)
                    if kind == "shift":
                        pe.wait_ge(shift_ready, half + 1)
                        nc.tensor.transpose(psum[0:SHIFT_PARTS * HG * TPC, bank, 0:P // 2].bitcast(BF16),
                                            shift[:, f].rearrange("p k n -> p (k n)"), ident_bf[:]).then_inc(scores_ready, 1)
                    else:
                        pe.wait_ge(sums_ready, half + 1)
                        transpose_tiles(sums[:, f, :].rearrange("p (t q) -> p t q", t=TPC), bank).then_inc(scores_ready, 1)

                def weighted_sums(w, buf, s, unit):
                    f, j, c0 = plan.steps[s]
                    if s == 0:
                        pe.wait_ge(vwin_ready, layer * WINDOWS + w + 1)
                    if s == plan.half_start[f]:
                        wait(pe, sums_ready, half_base + 2 * w + f)
                    pe.wait_ge(probs_ready, unit + 2)
                    for c in range(HG):
                        slot = (buf * 2 * plan.n + 2 * s + c // 2) % PROBS
                        at = (j * HG + c) * VH
                        ins = mm(psum[32 * c:32 * c + 32, 7, c0:], vwin[:, buf, at:at + 32], probs[:, slot, c % 2, c0:],
                                 start=(j == 0), stop=(s == plan.half_end[f]), tile_position=(0, 32 * c))
                    ins.then_inc(sums_done, 1)

                def transpose_ot(n, bank):
                    g = layer * CHUNKS + n
                    pe.wait_ge(ot_ready, g + 1)
                    wait(pe, xt_ready[1], g)
                    transpose_tiles(ot, bank).then_inc(ot_psum, 1)

                def project(n):
                    g = layer * CHUNKS + n
                    pe.wait_ge(ot_t_ready, g + 1)
                    wait(pe, x_mid, g)
                    for t in range(TPC):
                        ins = mm(psum[:, 6, t * P:(t + 1) * P], ot_t[:, t * P:(t + 1) * P], wout[:, layer, :], start=True, stop=True)
                    ins.then_inc(oproj_psum, 1)

                def transpose_ffn_xn(n, bank):
                    pe.wait_ge(xn_ready[1], layer * CHUNKS + n + 1)
                    transpose_tiles(ffn_xn, bank).then_inc(xt_psum[1], 1)

                def early_chunk(i):
                    if i == plan.project_at[0]:
                        pe.wait_ge(ring_free, job_base + plan.jobs_all)
                        transpose_ot(0, 4)
                    if i == plan.project_at[1]:
                        project(0)
                    if i == plan.project_at[2]:
                        transpose_ffn_xn(0, 4)

                def turn(w, buf, lap, steps, jobs, ends, index, static_index, unit, static_unit, between=None):
                    prev = (0, plan.turn - 1, unit - 2)
                    for i, ((dw, s), slots, end) in enumerate(zip(steps, jobs, ends)):
                        for part in range(4):
                            for jw, job in slots[part]:
                                run_job(lap + (buf + jw) // BUFS, (buf + jw) % BUFS, job, index, static_index)
                                index, static_index = index + 1, static_index + 1
                            if part < 2:
                                scores(w + dw, (buf + dw) % BUFS, s, part, unit + part, static_unit + part)
                            elif part == 2:
                                weighted_sums(w + prev[0], (buf + prev[0]) % BUFS, prev[1], prev[2])
                        prev = (dw, s, unit)
                        unit, static_unit = unit + 2, static_unit + 2
                        for jw, kind, f in end:
                            transpose_unit(w + jw, kind, f, unit, static_unit)
                            unit, static_unit = unit + 1, static_unit + 1
                        if between:
                            between(i)
                    return index, unit, prev

                index, unit = job_base, unit_base
                for kind, *what in plan.before:
                    if kind == "job":
                        run_job(0, 0, what[0], index, index)
                        index += 1
                        if layer == 0 and index in (4, 8, 12):
                            pe.wait_ge(wflt_ready, 1)
                            transpose_weights(index // 4 - 1)
                        continue
                    if layer == 0 and unit == 0:
                        pe.wait_ge(setup_ready, 4)
                    if kind == "shift":
                        transpose_unit(0, "shift", what[0], unit, unit)
                    else:
                        s, pair = what
                        scores(0, 0, s, pair, unit, unit)
                        if s and pair:
                            weighted_sums(0, 0, s - 1, unit - 3)
                    unit += 1
                windows(pe, lambda w, buf, lap: turn(w, buf, lap, plan.turn_steps, plan.turn_jobs, plan.turn_ends,
                                                w * plan.jobs_turn + index, buf * plan.jobs_turn + index,
                                                w * plan.units_turn + unit, buf * plan.units_turn + unit), WINDOWS - 1)
                last, last_buf = WINDOWS - 1, (WINDOWS - 1) % BUFS
                index, unit = index + last * plan.jobs_turn, unit + last * plan.units_turn
                index, unit, prev = turn(last, last_buf, last // BUFS, plan.turn_steps[:plan.n - plan.turn], plan.last_jobs, plan.last_ends,
                                         index, index, unit, unit, early_chunk)
                weighted_sums(last, last_buf, plan.n - 1, prev[2])
                transpose_unit(last, "norm", 1, unit, unit)
                pe.wait_ge(ring_free, job_base + plan.jobs_all)
                pe.wait_ge(probs_ready, unit_base + plan.units_all)

                def middle(n, buf, m):
                    out_stage, ffn_stage, _, qkv_stage = stages(layer, m)
                    g = layer * CHUNKS + n
                    if ffn_stage:
                        pe.wait_ge(xt_ready[1], g + 2)

                    def gate_up(c):
                        wait(pe, hid_ready, FB * (g + 1) + (0 if c < 2 else 1))
                        for k in range(2):
                            mm(psum[:, 2 + 2 * (c % 2) + k, :], wffn[:, k, c, :], ffn_xt[:], start=True, stop=True).then_inc(gate_up_psum, 1)

                    def down(tiles):
                        for t in tiles:
                            for c in range(FB):
                                ins = mm(psum[:, 7, t * P:(t + 1) * P], hid[:, c, t * P:(t + 1) * P], wffn[:, 2, c, :],
                                         start=(c == 0), stop=(c == FB - 1))
                        return ins

                    if out_stage:
                        transpose_ot(n + 2, 0)
                    if ffn_stage:
                        gate_up(0)
                    if out_stage:
                        project(n + 2)
                    if ffn_stage:
                        if layer == 0:
                            wait(pe, qk_ready, 2 * (g + CHUNKS))
                        gate_up(1)
                        gate_up(2)
                    if qkv_stage:
                        wait(pe, v_ready, g + CHUNKS)
                        transpose_xn(g + CHUNKS, buf, 1)
                    if qkv_stage:
                        if ffn_stage:
                            pe.wait_ge(hid_ready, FB * (g + 1) + 2)
                        qkv_products(1, g + CHUNKS, buf, 4, 1)
                    if ffn_stage:
                        pe.wait_ge(hid_ready, FB * (g + 2))
                        wait(pe, x_new, g + 1)
                        down(range(TPC - 1))
                    if out_stage:
                        transpose_ffn_xn(n + 2, 0)
                    if ffn_stage:
                        down(range(TPC - 1, TPC)).then_inc(down_psum, 1)

                pipeline(pe, middle, -1)
                pe.wait_ge(x_new, (layer + 1) * CHUNKS)


_INS = ["L0_attn_a_x", "L0_attn_a_Wqkv", "L0_attn_a_bqkv", "L0_attn_a_Wout", "L0_attn_a_bout",
        "L0_attn_b_W_qkv", "L0_attn_b_b_qkv", "L0_attn_b_W_out", "L0_attn_b_b_out",
        "L0_ffn_w_gate", "L0_ffn_w_up", "L0_ffn_w_down"]


def kernel(**inputs):
    import numpy as np
    import concourse.bacc as bacc
    from concourse.bass_utils import run_bass_kernel_spmd

    nc = bacc.Bacc("TRN2", target_bir_lowering=False, num_devices=1)
    arrays, args = {}, []
    for name in _INS:
        a = np.ascontiguousarray(inputs[name])
        arrays[f"in_{name}"] = a
        args.append(nc.dram_tensor(f"in_{name}", a.shape, mybir.dt.from_np(a.dtype), kind="ExternalInput").ap())
    out = nc.dram_tensor("out_x", (B, S, E), F32, kind="ExternalOutput").ap()
    transformer_pair_kernel(nc, *args, out)
    r = run_bass_kernel_spmd(nc, [arrays], core_ids=[0])
    return r.results[0]["out_x"]
```
